# Optimizing a Trainium2 kernel written in Bass

```python
import numpy as np
import jax
import jax.numpy as jnp

def _softmax(x, axis=-1):
    return jax.nn.softmax(x, axis=axis)

def _gelu(x):
    return jax.nn.gelu(x, approximate=True)

def _silu(x):
    return jax.nn.silu(x)

def _sigmoid(x):
    return jax.nn.sigmoid(x)

def _layernorm(x, axis=-1, eps=1e-05):
    m = jnp.mean(x, axis=axis, keepdims=True)
    v = jnp.var(x, axis=axis, keepdims=True)
    return (x - m) / jnp.sqrt(v + eps)

def _scatter_add(tgt, idx, src, axis=0):
    return tgt.at[idx].add(src)

def _segment_sum(src, seg, n):
    return jax.ops.segment_sum(src, seg, n)
kernel_name = 'mk_perceiver_d1_seqx_r4_77a807'

def setup_inputs(seed: int=0):
    np.random.seed(seed)
    _w = jnp.asarray

    def _rec_inputs():
        import jax
        import jax.numpy as jnp
        _rk = jax.random.key(seed)
        x = 7.22e-05 + 1 * jax.random.normal(jax.random.fold_in(_rk, 1), (64, 32, 256), jnp.float32)
        _lenS = 32 - jax.random.randint(jax.random.fold_in(_rk, 7), (64,), 0, max(1, 32 // 4) + 1, jnp.int32)
        _lenS2 = 257 - jax.random.randint(jax.random.fold_in(_rk, 8), (64,), 0, max(1, 257 // 4) + 1, jnp.int32)
        _ctx_768P = jax.random.normal(jax.random.fold_in(_rk, 11), (64, 16, 192), jnp.float32)
        _ctx_768c = jax.random.dirichlet(jax.random.fold_in(_rk, 511), 0.3 * jnp.ones((16,), jnp.float32), (64, 257))
        _ctx_768t = jnp.einsum('bsk,bkd->bsd', _ctx_768c, _ctx_768P)
        _ctx_768t = _ctx_768t * jax.lax.rsqrt(jnp.mean(jnp.square(_ctx_768t)) + 1e-12) * 0.953939
        ctx_768 = -0.000191848 + 0.999787 * (_ctx_768t + 0.3 * jax.random.normal(jax.random.fold_in(_rk, 611), (64, 257, 192), jnp.float32))
        _validS = jnp.arange(32)[None, :] < _lenS[:, None]
        _validS2 = jnp.arange(257)[None, :] < _lenS2[:, None]
        _causal = jnp.tril(jnp.ones((32, 32), dtype=bool))
        mask_1x1xSxS2_bk0 = jnp.logical_not(jnp.broadcast_to(_validS2[0:1, None, None, :], (1, 1, 32, 257)))
        return (x, ctx_768, mask_1x1xSxS2_bk0)
    x, ctx_768, mask_1x1xSxS2_bk0 = _rec_inputs()

    def _L0_xattn_setup():
        import jax, jax.numpy as jnp
        import numpy as np
        B, T, Q_DIM, KV_DIM = (4, 512, 256, 192)
        HEADS, DIM_HEAD = (16, 64)
        INNER = HEADS * DIM_HEAD
        NUM_FRAMES, NUM_PATCHES = (8, 64)
        LN_EPS = 1e-05

        def diagonal_frame_mask(num_patches, num_frames):
            fid = np.repeat(np.arange(num_frames), num_patches)
            m = fid[:, None] == fid[None, :]
            return jnp.asarray(m[None, None])
        key = jax.random.key(seed)
        ks = jax.random.split(key, 6)
        s = lambda d: 1.0 / np.sqrt(d)
        return {'x': jax.random.normal(ks[0], (B, T, Q_DIM), jnp.float32), 'context': jax.random.normal(ks[1], (B, T, KV_DIM), jnp.float32), 'ln_gamma': jnp.ones((Q_DIM,), jnp.float32), 'ln_beta': jnp.zeros((Q_DIM,), jnp.float32), 'Wq': jax.random.normal(ks[2], (Q_DIM, INNER), jnp.float32) * s(Q_DIM), 'Wkv': jax.random.normal(ks[3], (KV_DIM, 2 * INNER), jnp.float32) * s(KV_DIM), 'Wo': jax.random.normal(ks[4], (INNER, Q_DIM), jnp.float32) * s(INNER), 'bo': jnp.zeros((Q_DIM,), jnp.float32), 'mask': diagonal_frame_mask(NUM_PATCHES, NUM_FRAMES)}
    _L0_xattn_all = _L0_xattn_setup()
    _L0_xattn_in = {k: v for k, v in _L0_xattn_all.items() if k in ('ln_gamma', 'ln_beta', 'Wq', 'Wkv', 'Wo', 'bo')}
    del _L0_xattn_all

    def _L0_attn_setup():
        import jax, jax.numpy as jnp
        import numpy as np
        D_MODEL = 256
        NHEAD = 16
        HEAD_DIM = D_MODEL // NHEAD
        SCALE = HEAD_DIM ** (-0.5)
        EPS_LN = 1e-05
        key = jax.random.key(seed)
        ks = jax.random.split(key, 7)
        B, T, D = (2, 512, D_MODEL)
        x = jax.random.normal(ks[0], (B, T, D), dtype=jnp.float32)
        ln_gamma = jnp.ones((D,), dtype=jnp.float32)
        ln_beta = jnp.zeros((D,), dtype=jnp.float32)
        s = 1.0 / np.sqrt(D)
        W_qkv = jax.random.uniform(ks[1], (D, 3 * D), minval=-s, maxval=s, dtype=jnp.float32)
        b_qkv = jax.random.uniform(ks[2], (3 * D,), minval=-s, maxval=s, dtype=jnp.float32)
        W_proj = jax.random.uniform(ks[3], (D, D), minval=-s, maxval=s, dtype=jnp.float32)
        b_proj = jax.random.uniform(ks[4], (D,), minval=-s, maxval=s, dtype=jnp.float32)
        return {'x': x, 'ln_gamma': ln_gamma, 'ln_beta': ln_beta, 'W_qkv': W_qkv, 'b_qkv': b_qkv, 'W_proj': W_proj, 'b_proj': b_proj}
    _L0_attn_all = _L0_attn_setup()
    _L0_attn_in = {k: v for k, v in _L0_attn_all.items() if k in ('ln_gamma', 'ln_beta', 'W_qkv', 'b_qkv', 'W_proj', 'b_proj')}
    del _L0_attn_all

    def _L0_ffn_setup():
        import jax, jax.numpy as jnp
        import numpy as np
        DIM = 256

        def _reference_tuple_inner(x, W_r, W_k, W_v, mu_r, mu_k):
            B, T, C = x.shape
            x_prev = jnp.concatenate([jnp.zeros((B, 1, C), x.dtype), x[:, :-1, :]], axis=1)
            xr = mu_r * x + (1.0 - mu_r) * x_prev
            xk = mu_k * x + (1.0 - mu_k) * x_prev
            r = jax.nn.sigmoid(jnp.einsum('btc,dc->btd', xr, W_r))
            k = jnp.einsum('btc,dc->btd', xk, W_k)
            k_act = jnp.square(jax.nn.relu(k))
            out = r * jnp.einsum('btc,dc->btd', k_act, W_v)
            new_state = x[:, -1, :]
            return (out, new_state)
        key = jax.random.key(seed)
        ks = jax.random.split(key, 6)
        B, T, C = (8, 512, DIM)
        x = jax.random.normal(ks[0], (B, T, C), dtype=jnp.float32)
        s = 1.0 / np.sqrt(C)
        W_r = jax.random.uniform(ks[1], (C, C), jnp.float32, -s, s)
        W_k = jax.random.uniform(ks[2], (C, C), jnp.float32, -s, s)
        W_v = jax.random.uniform(ks[3], (C, C), jnp.float32, -s, s)
        mu_r = jax.random.uniform(ks[4], (C,), jnp.float32)
        mu_k = jax.random.uniform(ks[5], (C,), jnp.float32)
        return {'x': x, 'W_r': W_r, 'W_k': W_k, 'W_v': W_v, 'mu_r': mu_r, 'mu_k': mu_k}
    _L0_ffn_all = _L0_ffn_setup()
    _L0_ffn_in = {k: v for k, v in _L0_ffn_all.items() if k in ('W_r', 'W_k', 'W_v', 'mu_r', 'mu_k')}
    del _L0_ffn_all
    return {'x': x, 'ctx_768': ctx_768, 'mask_1x1xSxS2_bk0': mask_1x1xSxS2_bk0, 'L0_xattn_ln_gamma': _L0_xattn_in['ln_gamma'], 'L0_xattn_ln_beta': _L0_xattn_in['ln_beta'], 'L0_xattn_Wq': _L0_xattn_in['Wq'], 'L0_xattn_Wkv': _L0_xattn_in['Wkv'], 'L0_xattn_Wo': _L0_xattn_in['Wo'], 'L0_xattn_bo': _L0_xattn_in['bo'], 'L0_attn_ln_gamma': _L0_attn_in['ln_gamma'], 'L0_attn_ln_beta': _L0_attn_in['ln_beta'], 'L0_attn_W_qkv': _L0_attn_in['W_qkv'], 'L0_attn_b_qkv': _L0_attn_in['b_qkv'], 'L0_attn_W_proj': _L0_attn_in['W_proj'], 'L0_attn_b_proj': _L0_attn_in['b_proj'], 'L0_ffn_W_r': _L0_ffn_in['W_r'], 'L0_ffn_W_k': _L0_ffn_in['W_k'], 'L0_ffn_W_v': _L0_ffn_in['W_v'], 'L0_ffn_mu_r': _L0_ffn_in['mu_r'], 'L0_ffn_mu_k': _L0_ffn_in['mu_k']}

def reference(x, ctx_768, mask_1x1xSxS2_bk0, L0_xattn_ln_gamma, L0_xattn_ln_beta, L0_xattn_Wq, L0_xattn_Wkv, L0_xattn_Wo, L0_xattn_bo, L0_attn_ln_gamma, L0_attn_ln_beta, L0_attn_W_qkv, L0_attn_b_qkv, L0_attn_W_proj, L0_attn_b_proj, L0_ffn_W_r, L0_ffn_W_k, L0_ffn_W_v, L0_ffn_mu_r, L0_ffn_mu_k):
    import jax
    import jax.numpy as jnp

    def _L0_xattn_ref(x, context, ln_gamma, ln_beta, Wq, Wkv, Wo, bo, mask):
        import jax, jax.numpy as jnp
        import numpy as np
        B, T, Q_DIM, KV_DIM = (4, 512, 256, 192)
        HEADS, DIM_HEAD = (16, 64)
        INNER = HEADS * DIM_HEAD
        NUM_FRAMES, NUM_PATCHES = (8, 64)
        LN_EPS = 1e-05

        def diagonal_frame_mask(num_patches, num_frames):
            fid = np.repeat(np.arange(num_frames), num_patches)
            m = fid[:, None] == fid[None, :]
            return jnp.asarray(m[None, None])
        mu = jnp.mean(x, axis=-1, keepdims=True)
        var = jnp.mean(jnp.square(x - mu), axis=-1, keepdims=True)
        xn = (x - mu) * jax.lax.rsqrt(var + LN_EPS) * ln_gamma + ln_beta
        scale = DIM_HEAD ** (-0.5)
        q = xn @ Wq
        kv = context @ Wkv
        k, v = jnp.split(kv, 2, axis=-1)
        split_heads = lambda t: t.reshape(t.shape[0], t.shape[1], HEADS, DIM_HEAD).transpose(0, 2, 1, 3)
        q, k, v = (split_heads(q), split_heads(k), split_heads(v))
        dots = jnp.einsum('bhnd,bhmd->bhnm', q, k) * scale
        dots = jnp.where(mask, dots, -jnp.inf)
        attn = jax.nn.softmax(dots, axis=-1)
        out = jnp.einsum('bhnm,bhmd->bhnd', attn, v)
        out = out.transpose(0, 2, 1, 3).reshape(x.shape[0], x.shape[1], INNER)
        return out @ Wo + bo

    def _L0_attn_ref(x, ln_gamma, ln_beta, W_qkv, b_qkv, W_proj, b_proj):
        import jax, jax.numpy as jnp
        import numpy as np
        D_MODEL = 256
        NHEAD = 16
        HEAD_DIM = D_MODEL // NHEAD
        SCALE = HEAD_DIM ** (-0.5)
        EPS_LN = 1e-05
        B, T, D = x.shape
        h, dh = (NHEAD, HEAD_DIM)
        mu = jnp.mean(x, axis=-1, keepdims=True)
        var = jnp.mean(jnp.square(x - mu), axis=-1, keepdims=True)
        x_n = (x - mu) * jax.lax.rsqrt(var + EPS_LN) * ln_gamma + ln_beta
        qkv = x_n @ W_qkv + b_qkv
        q, k, v = jnp.split(qkv, 3, axis=-1)
        q = q.reshape(B, T, h, dh).transpose(0, 2, 1, 3)
        k = k.reshape(B, T, h, dh).transpose(0, 2, 1, 3)
        v = v.reshape(B, T, h, dh).transpose(0, 2, 1, 3)
        scores = jnp.einsum('bhqd,bhkd->bhqk', q, k) * SCALE
        scores = scores - jnp.max(scores, axis=-1, keepdims=True)
        attn = jnp.exp(scores)
        attn = attn / jnp.maximum(jnp.sum(attn, axis=-1, keepdims=True), 1e-12)
        ctx = jnp.einsum('bhqk,bhkd->bhqd', attn, v)
        ctx = ctx.transpose(0, 2, 1, 3).reshape(B, T, D)
        return ctx @ W_proj + b_proj

    def _L0_ffn_ref(x, W_r, W_k, W_v, mu_r, mu_k):
        import jax, jax.numpy as jnp
        import numpy as np
        DIM = 256

        def _reference_tuple_inner(x, W_r, W_k, W_v, mu_r, mu_k):
            B, T, C = x.shape
            x_prev = jnp.concatenate([jnp.zeros((B, 1, C), x.dtype), x[:, :-1, :]], axis=1)
            xr = mu_r * x + (1.0 - mu_r) * x_prev
            xk = mu_k * x + (1.0 - mu_k) * x_prev
            r = jax.nn.sigmoid(jnp.einsum('btc,dc->btd', xr, W_r))
            k = jnp.einsum('btc,dc->btd', xk, W_k)
            k_act = jnp.square(jax.nn.relu(k))
            out = r * jnp.einsum('btc,dc->btd', k_act, W_v)
            new_state = x[:, -1, :]
            return (out, new_state)
        return _reference_tuple_inner(x, W_r, W_k, W_v, mu_r, mu_k)[0]
    x = x + _L0_xattn_ref(_layernorm(x, axis=-1), ctx_768, L0_xattn_ln_gamma, L0_xattn_ln_beta, L0_xattn_Wq, L0_xattn_Wkv, L0_xattn_Wo, L0_xattn_bo, mask_1x1xSxS2_bk0)
    x = x + _L0_attn_ref(_layernorm(x, axis=-1), L0_attn_ln_gamma, L0_attn_ln_beta, L0_attn_W_qkv, L0_attn_b_qkv, L0_attn_W_proj, L0_attn_b_proj)
    x = x + _L0_ffn_ref(_layernorm(x, axis=-1), L0_ffn_W_r, L0_ffn_W_k, L0_ffn_W_v, L0_ffn_mu_r, L0_ffn_mu_k)
    return x

_drawn_inputs = setup_inputs


def setup_inputs(seed=0):
    import zlib

    import numpy as np

    out = dict(_drawn_inputs(seed))
    spreads = {'L0_xattn_ln_gamma': (1.0, 0.2),
     'L0_xattn_ln_beta': (0.0, 0.323),
     'L0_xattn_bo': (0.0, 0.1),
     'L0_attn_ln_gamma': (1.0, 0.577),
     'L0_attn_ln_beta': (0.0, 0.1)}
    factors = {'L0_attn_b_qkv': 2.778, 'L0_ffn_W_r': 3.276, 'L0_ffn_mu_r': 7.965}
    for name, (base, spread) in spreads.items():
        noise = np.random.default_rng([zlib.crc32(name.encode()), seed]).standard_normal(out[name].shape)
        drawn = base * np.exp(spread * noise) if base else spread * noise
        out[name] = jnp.asarray(drawn.astype(out[name].dtype))
    for name, factor in factors.items():
        out[name] = (out[name] * factor).astype(out[name].dtype)
    return out
```

```python
from contextlib import ExitStack

import concourse.bass as bass
from concourse import mybir

ALU = mybir.AluOpType
ACT = mybir.ActivationFunctionType
AX = mybir.AxisListType
F32 = mybir.dt.float32
I32 = mybir.dt.int32
U8 = mybir.dt.uint8

P = 128
NB, NQ, DM = 64, 32, 256
NK, DC = 257, 192
NKF = 256
NH, DH = 16, 64
SH, SD = 16, 16
GB = 8
NG = NB // GB
TOK = GB * NQ
XT_TILES = TOK // P
HT = 4
NT = NH // HT
NPAIR = NH // 2
NCTX = 4
EPS = 1e-5
BIG = 3.0e38
MASKED = 1.0e30
EXP_MAX = -87.0
RSQRT_SEED = float(0x5F3759DF)
NEWTON = 3

AUX = [f"CT{j}" for j in range(GB)] + ["LV0", "LV1", "LT"]
PRE = ["XT", "Q0", "Q1", "Q2", "Q3"]
POST = ["OT0", "OT1", "OT2", "OT3", "WO0", "WO1", "T2", "QT", "KT", "VR", "SC0", "SC1",
        "PT0", "PT1", "PV", "T4", "PJ", "T3", "FR", "FK", "FV"]
GAPS = [
    [["XB", "OT0"], [], ["OT1"], [], ["OT2"], [], ["OT3"], []],
    [["WO0"], [], [], ["WO1"], [], ["LN1"], [], []],
    [["T2"], [], ["XT"], [], ["QT"], ["Q0"], [], ["KT"]],
    [[], ["VR"], [], ["SC0"], ["Q1"], ["SC1"], ["SM0"], []],
    [["SM1"], ["Q2"], [], ["PT0"], [], ["PT1"], [], ["PV"]],
    [[], ["Q3"], ["T4"], [], ["PJ"], [], [], []],
    [["T3"], ["MIX"], [], [], ["FR"], ["LV0"], ["FK"], []],
    [["LV1"], ["SG"], [], ["FV"], [], [], [], []],
]
LN_LINKS = 5 + 3 * NEWTON


def perceiver_layer(nc, x, ctx_in, mask, g1, be1, Wq, Wkv, Wo, bo, g2, be2, Wqkv, bqkv, Wproj, bproj,
                    Wr, Wk, Wv, mur, muk, out):
    with ExitStack() as es:
        def sb(name, shape, dt=F32):
            return es.enter_context(nc.sbuf_tensor(name, shape, dt))

        def sem(name):
            return es.enter_context(nc.semaphore(name))

        def psum(name):
            return es.enter_context(nc.psum_tensor(name, [P, 512], F32))

        wq = sb("wq", [P, 2, NH * DH])
        nwk = sb("nwk", [P, NH * DC + 64])
        wvn = sb("wvn", [P, 2, NH * DH])
        wvb = sb("wvb", [P, NPAIR, P])
        wo = sb("wo", [P, NPAIR, DM])
        wqkv = sb("wqkv", [P, 2, 3 * DM])
        wproj = sb("wproj", [P, 2, DM])
        wrT = sb("wrT", [P, 2, DM])
        wkT = sb("wkT", [P, 2, DM])
        wvT = sb("wvT", [P, 2, DM])
        cols = sb("cols", [P, 8, 2])
        G1, B1, G2, B2, MUR, MUK, MUR1, MUK1 = range(8)
        bcol = sb("bcol", [P, 6])
        bo_row = sb("bo_row", [P, DM])
        bp_row = sb("bp_row", [P, DM])
        ident = sb("ident", [P, P])
        mraw = sb("mraw", [P, NK], U8)
        mbias = sb("mbias", [P, NK])
        poison = sb("poison", [P, 2])
        headm = sb("headm", [P, 8])
        seqm = sb("seqm", [NQ, GB])
        leftm = sb("leftm", [P, 4, 4])
        left = sb("left", [P, 2, NB])
        leftr = sb("leftr", [P, 2, 16, GB])
        cx_in = [sb(f"cx_in{r}", [P, 2, 256]) for r in range(NCTX)]
        cT = [sb(f"cT{r}", [P, 2, NK]) for r in range(2)]
        qk = sb("qk", [P, 2, GB, NH * NQ])
        sm = sb("sm", [P, NT, NK])
        nmx = sb("nmx", [P, 2, NT])
        ssum = sb("ssum", [P, 2, NT])
        rsum = sb("rsum", [P, 2, NT])
        pr = [sb(f"pr{r}", [P, NT, NK]) for r in range(2)]
        prT = sb("prT", [P, 2, NH * NQ])
        lastp = sb("lastp", [P, NT, GB])
        spread = sb("spread", [P, GB, NQ])
        lv = sb("lv", [P, NH, DH])
        acm = sb("acm", [P, NH, TOK])
        act_ = sb("act_", [P, NPAIR, TOK])
        xn = sb("xn", [P, 2, DM])
        xnT = sb("xnT", [P, 2, TOK])
        qT = sb("qT", [P, NPAIR, TOK])
        xb = sb("xb", [P, 2, DM])
        x1 = sb("x1", [P, 2, DM])
        x2 = x1
        hn = sb("hn", [P, 2, DM])
        hT = sb("hT", [P, 2, TOK])
        q2T = sb("q2T", [P, 2, TOK])
        kM = sb("kM", [P, 2, 8, TOK])
        sc = sb("sc", [P, 2, SH, NQ])
        smx = sb("smx", [P, 2, SH])
        ssm = sb("ssm", [P, 2, SH])
        rs2 = sb("rs2", [P, 2, SH])
        vb = sb("vb", [P, GB, 4, 4, SD])
        cv, cvT = hT, q2T
        x3T = sb("x3T", [P, 2, GB, NQ + 1])
        er = sb("er", [P, 2, DM])
        yo = sb("yo", [P, 2, DM])
        st = sb("st", [P, 3, 2, 6])
        mv = sb("mv", [P, 3, 2, 2])
        lw = sb("lw", [P, 3, 4, 2])
        li = sb("li", [P, 3, 2], I32)

        stage = kM[:].rearrange("p a b c -> p (a b c)")
        wk_main, wk_tail = stage[:, 0:1024], stage[0:64, 1024:2048]
        p2T = stage[:, 0:1024].rearrange("p (a c q) -> p a c q", a=2, c=4)
        mixt = stage[:, 1024:2048].rearrange("p (s t) -> p s t", s=4)
        mix = stage[:, 2048:3072].rearrange("p (s t) -> p s t", s=4)
        kr = stage[:, 3072:3584].rearrange("p (k t) -> p k t", k=2)
        ka = stage[:, 3584:4096].rearrange("p (k t) -> p k t", k=2)
        ffn_in = [stage[:, 2048 + 512 * n:2560 + 512 * n].rearrange("p (k c) -> p k c", k=2) for n in range(3)]
        left_in = stage[0:NB, 3584:3584 + DC]

        score = [psum("score0"), psum("score1")]
        probT, ac_main, ac_tail, aux, pre, post = (psum(n) for n in ("probT", "ac_main", "ac_tail", "aux", "pre", "post"))
        banks = [score[0], score[1], probT, ac_main, ac_tail, aux, pre, post]

        consts_made, ident_made, zeroed = sem("consts_made"), sem("ident_made"), sem("zeroed")
        weights_in, staged_in, mask_in, small_in = sem("weights_in"), sem("staged_in"), sem("mask_in"), sem("small_in")
        setup_full, setup_copied = sem("setup_full"), sem("setup_copied")
        waits_passed = sem("waits_passed")
        x_in, xres_in, stored = sem("x_in"), sem("xres_in"), sem("stored")
        ctx_loaded = [sem(f"ctx_loaded{r}") for r in range(NCTX)]
        left_ready, col_ready = sem("left_ready"), sem("col_ready")
        aux_full, aux_free = sem("aux_full"), sem("aux_free")
        pre_full, pre_free = sem("pre_full"), sem("pre_free")
        post_full, post_free = sem("post_full"), sem("post_free")
        qk_full, qk_copied_act, qk_copied_dve = sem("qk_full"), sem("qk_copied_act"), sem("qk_copied_dve")
        scores_done, scores_masked, exp_done = sem("scores_done"), sem("scores_masked"), sem("exp_done")
        recip_done, probs_ready, lastp_ready = sem("recip_done"), sem("probs_ready"), sem("lastp_ready")
        probT_full, probT_copied = sem("probT_full"), sem("probT_copied")
        ac_done, acm_copied, act_copied = sem("ac_done"), sem("acm_copied"), sem("act_copied")
        ln_link = [sem(f"ln_link{n}") for n in range(3)]
        ln_ready = [sem(f"ln_ready{n}") for n in range(3)]
        xb_ready, x1b_ready, smx_ready = sem("xb_ready"), sem("x1b_ready"), sem("smx_ready")
        sexp_done, ssum_done, srecip_done, p2_ready = sem("sexp_done"), sem("ssum_done"), sem("srecip_done"), sem("p2_ready")
        half_mixed, mixed = sem("half_mixed"), sem("mixed")
        ka_ready, er_exp, er_one, r_ready = sem("ka_ready"), sem("er_exp"), sem("er_one"), sem("r_ready")
        y_ready = sem("y_ready")

        x_rows = x.rearrange("b n c -> (b n) c")
        out_rows = out.rearrange("b n c -> (b n) c")

        def token_rows(t, g):
            return t[bass.ds(g * TOK, TOK), :].rearrange("(a p) c -> p a c", p=P)

        def after(eng, s, value):
            if isinstance(value, int) and value <= 0:
                return
            eng.wait_ge(s, value)

        def alone(eng):
            eng.sem_inc(waits_passed)

        def nth(jobs, name, g):
            return g * len(jobs) + jobs.index(name) + 1

        def groups(eng, group):
            group(0, True, False)
            group(1, True, True)
            with eng.Fori(2, NG - 1) as g:
                group(g, True, True)
            group(NG - 1, False, True)

        def jobs_at(j, piece, has_pre, has_post):
            for name in GAPS[j][piece]:
                if name in PRE or name == "LN1":
                    if has_pre:
                        yield name
                elif name in AUX:
                    yield name
                elif has_post:
                    yield name

        es.enter_context(nc.allow_non_contiguous_dma(reason="per-channel vectors, one element to a partition"))
        block = es.enter_context(nc.Block())

        N_WEIGHTS, N_STAGED, N_SMALL, N_SETUP = 8, 6, 9, 9

        @block.sync
        def _(sp):
            def load_ctx(b, slot):
                sp.dma_start(cx_in[slot][:, :, 0:DC],
                             ctx_in[bass.ds(b, 1), 0:NKF, :].rearrange("o (k p) c -> p (o k) c", p=P)).then_inc(ctx_loaded[slot], 16)

            def column(v):
                return v.rearrange("(k p) -> p k", p=P)

            sp.dma_start(xn[:], token_rows(x_rows, 0)).then_inc(x_in, 16)
            sp.dma_start(wk_main, Wkv[0:P, 0:NH * DH]).then_inc(staged_in, 16)
            sp.dma_start(wk_tail, Wkv[P:DC, 0:NH * DH]).then_inc(staged_in, 16)
            sp.dma_start(left_in, ctx_in[:, NKF, :]).then_inc(staged_in, 16)
            for n, w in enumerate((Wr, Wk, Wv)):
                sp.dma_start(ffn_in[n], w.rearrange("(k p) c -> p k c", p=P)).then_inc(staged_in, 16)
            for n, v in ((G1, g1), (B1, be1), (G2, g2), (B2, be2), (MUR, mur), (MUK, muk)):
                sp.dma_start(cols[:, n, :], column(v)).then_inc(small_in, 16)
            sp.dma_start(bcol[:], column(bqkv)).then_inc(small_in, 16)
            sp.dma_start(wq[:], Wq.rearrange("(k p) n -> p k n", p=P)).then_inc(weights_in, 16)
            for r in range(4):
                sp.dma_start(mraw[r * NQ:(r + 1) * NQ, :], mask[0, 0, :, :]).then_inc(mask_in, 16)
            for r in range(NCTX):
                load_ctx(r, r)
            sp.wait_ge(zeroed, 3)
            wv_all = Wkv[:, NH * DH:2 * NH * DH]
            sp.dma_start(wvn[:, 0, :], wv_all[0:P, :]).then_inc(weights_in, 16)
            sp.dma_start(wvn[0:64, 1, :], wv_all[P:DC, :]).then_inc(weights_in, 16)
            tails = wv_all[P:DC, :].rearrange("c (n r d) -> c n r d", r=2, d=DH)
            for r in range(2):
                sp.dma_start(wvb[r * 64:r * 64 + 64, :, r * 64:r * 64 + 64], tails[:, :, r, :]).then_inc(small_in, 16)
            sp.dma_start(wo[:], Wo.rearrange("(k p) n -> p k n", p=P)).then_inc(weights_in, 16)
            sp.dma_start(wqkv[:], Wqkv.rearrange("(k p) n -> p k n", p=P)).then_inc(weights_in, 16)
            sp.dma_start(wproj[:], Wproj.rearrange("(k p) n -> p k n", p=P)).then_inc(weights_in, 16)
            sp.dma_start(bo_row[:], bo.partition_broadcast(P)).then_inc(weights_in, 16)
            sp.dma_start(bp_row[:], bproj.partition_broadcast(P)).then_inc(weights_in, 16)

            def store(g):
                sp.wait_ge(y_ready, g + 1)
                sp.dma_start(token_rows(out_rows, g), yo[:]).then_inc(stored, 16)

            def load_residual(g):
                after(sp, y_ready, g)
                sp.dma_start(xb[:], token_rows(x_rows, g)).then_inc(xres_in, 16)

            def group(g, has_pre, has_post):
                if has_pre:
                    sp.wait_ge(pre_full, nth(PRE, "XT", g))
                    sp.dma_start(xn[:], token_rows(x_rows, g + 1)).then_inc(x_in, 16)
                if has_post:
                    load_residual(g - 1)
                for j in range(GB if has_pre else GB - NCTX):
                    sp.wait_ge(ac_done, g * GB + j + 1)
                    load_ctx(g * GB + j + NCTX, j % NCTX)
                if has_post:
                    store(g - 1)

            groups(sp, group)
            load_residual(NG - 1)
            store(NG - 1)
            sp.wait_ge(stored, 16 * NG)

        @block.gpsimd
        def _(pool):
            pool.memset(ident[:], 0.0).then_inc(ident_made, 1)
            pool.memset(wvn[:, 1, :], 0.0).then_inc(zeroed, 1)
            pool.memset(wvb[:], 0.0).then_inc(zeroed, 1)
            pool.memset(nwk[:], 0.0).then_inc(zeroed, 1)
            pool.wait_ge(ident_made, 1)
            pool.affine_select(out=ident[:], in_=ident[:], compare_op=ALU.not_equal, fill=1.0, base=0,
                               pattern=[[-1, P]], channel_multiplier=1).then_inc(ident_made, 1)
            pool.memset(left[:], 0.0).then_inc(zeroed, 1)
            for r in range(NCTX):
                pool.memset(cx_in[r][:, :, DC:256], 0.0).then_inc(zeroed, 1)
            pool.memset(vb[:], 0.0).then_inc(zeroed, 1)
            pool.memset(x3T[:, :, :, 0], 0.0).then_inc(zeroed, 1)

            def columns(g, j):
                after(pool, scores_done, g * GB * NT + (j - 1) * NT)
                alone(pool)
                pool.tensor_copy(cT[j % 2][:, :, NKF], leftr[:, :, 0, j]).then_inc(col_ready, 1)

            def normalise(g, j, half):
                pool.wait_ge(recip_done, 2 * (g * GB + j) + half + 1)
                alone(pool)
                for t in (2 * half, 2 * half + 1):
                    p = pr[j % 2][:, t, :]
                    last = pool.tensor_scalar(p, p, rsum[:, j % 2, t:t + 1], poison[:, 0:1], ALU.mult, ALU.mult)
                last.then_inc(probs_ready, 1)
                if half == 1:
                    if j == 0:
                        after(pool, aux_full, g * len(AUX))
                    pool.wait_ge(probs_ready, 2 * (g * GB + j) + 2)
                    alone(pool)
                    pool.tensor_copy(lastp[:, :, j], pr[j % 2][:, :, NKF]).then_inc(lastp_ready, 1)

            def job(name, g):
                if name == "XB":
                    pool.wait_ge(xres_in, 16 * (g + 1))
                    for a in range(2):
                        last = pool.tensor_tensor(xb[:, a, :], xb[:, a, :], bo_row[:], ALU.add)
                    last.then_inc(xb_ready, 1)
                elif name == "T2":
                    pool.wait_ge(post_free, nth(POST, "WO1", g))
                    for a in range(2):
                        last = pool.tensor_tensor(xb[:, a, :], x1[:, a, :], bp_row[:], ALU.add)
                    last.then_inc(x1b_ready, 1)
                elif name in ("SM0", "SM1"):
                    a = int(name[2])
                    pool.wait_ge(srecip_done, 2 * g + a + 1)
                    pool.tensor_tensor(sc[:, a], sc[:, a], rs2[:, a, :].unsqueeze(2).broadcast_to([P, SH, NQ]),
                                       ALU.mult).then_inc(p2_ready, 1)
                elif name == "FK":
                    pool.wait_ge(post_free, nth(POST, "FK", g))
                    pool.tensor_tensor(ka, kr, kr, ALU.mult).then_inc(ka_ready, 1)
                elif name == "FV":
                    pool.wait_ge(post_free, nth(POST, "FV", g))
                    after(pool, stored, 16 * g)
                    pool.tensor_tensor(yo[:], er[:], x2[:], ALU.add).then_inc(y_ready, 1)

            def group(g, has_pre, has_post):
                after(pool, aux_full, g * len(AUX))
                after(pool, col_ready, g * GB)
                alone(pool)
                pool.tensor_copy(leftr[:], left[:, :, bass.ds(g * GB, GB)].unsqueeze(2).broadcast_to([P, 2, 16, GB])).then_inc(left_ready, 1)
                pool.wait_ge(left_ready, g + 1)
                columns(g, 0)
                for j in range(GB):
                    for piece in range(8):
                        if piece == 0 and j < GB - 1:
                            columns(g, j + 1)
                        if piece == 2 and j > 0:
                            normalise(g, j - 1, 1)
                        if piece == 5:
                            normalise(g, j, 0)
                        for name in jobs_at(j, piece, has_pre, has_post):
                            job(name, g - 1)
                normalise(g, GB - 1, 1)

            pool.wait_ge(setup_copied, N_SETUP)
            pool.wait_ge(consts_made, 7)
            pool.wait_ge(weights_in, 16 * N_WEIGHTS)
            groups(pool, group)
            for j in range(GB):
                for piece in range(8):
                    for name in jobs_at(j, piece, False, True):
                        if name not in AUX:
                            job(name, NG - 1)

        @block.tensor
        def _(pe):
            pe.wait_ge(ident_made, 2)
            pe.wait_ge(staged_in, 16 * N_STAGED)
            pe.transpose(banks[0][:, 0:NB], left_in[:, 0:P], ident[0:NB, 0:NB])
            pe.transpose(banks[0][0:64, NB:2 * NB], left_in[:, P:DC], ident[0:NB, 0:NB]).then_inc(setup_full, 1)
            for n in range(4):
                for i in range(2):
                    pair = slice((2 * n + i) * P, (2 * n + i + 1) * P)
                    pe.transpose(banks[1 + n][:, i * DC:i * DC + P], wk_main[:, pair], ident[:])
                    last = pe.transpose(banks[1 + n][:, i * DC + P:(i + 1) * DC], wk_tail[:, pair], ident[0:64, 0:64])
                last.then_inc(setup_full, 1)
            for n in range(3):
                for kd in range(2):
                    for kc in range(2):
                        last = pe.transpose(banks[5 + n][:, kc * DM + kd * P:kc * DM + (kd + 1) * P],
                                            ffn_in[n][:, kd, kc * P:(kc + 1) * P], ident[:])
                last.then_inc(setup_full, 1)
            pe.wait_ge(setup_copied, N_SETUP)
            pe.wait_ge(zeroed, 10)
            pe.wait_ge(weights_in, 16 * N_WEIGHTS)
            pe.wait_ge(small_in, 16 * N_SMALL)

            def transposes(bank, src):
                for a in range(2):
                    for k in range(2):
                        last = pe.transpose(bank[:, k * TOK + a * P:k * TOK + (a + 1) * P], src[:, a, k * P:(k + 1) * P], ident[:])
                return last

            def pre_job(name, g):
                after(pe, pre_free, nth(PRE, name, g) - 1)
                if name == "XT":
                    pe.wait_ge(ln_ready[0], g + 1)
                    last = transposes(pre, xn)
                else:
                    n = int(name[1])
                    for i in range(2):
                        for k in range(2):
                            last = pe.matmul(pre[:, i * TOK:(i + 1) * TOK], wq[:, k, (2 * n + i) * P:(2 * n + i + 1) * P],
                                             xnT[:, k, :], start=(k == 0), stop=(k == 1))
                last.then_inc(pre_full, 1)

            def qk_job(h, g):
                bank = score[h % 2]
                if h == 0:
                    after(pe, scores_masked, g * GB * NT)
                    pe.wait_ge(pre_free, nth(PRE, "Q3", g))
                if h >= 2:
                    copied = (qk_copied_act, qk_copied_dve)[h % 2]
                    pe.wait_ge(copied, g * (NH // 2) + h // 2)
                for k in range(2):
                    last = pe.matmul(bank[:, k * TOK:(k + 1) * TOK], nwk[:, h * DC + k * P:h * DC + (k + 1) * P],
                                     qT[:, h // 2, :], start=True, stop=True)
                last.then_inc(qk_full, 1)

            def aux_job(name, g):
                after(pe, aux_free, nth(AUX, name, g) - 1)
                if name[:2] == "CT":
                    j = int(name[2])
                    pe.wait_ge(ctx_loaded[j % NCTX], g * 16 * (GB // NCTX) + 16 * (j // NCTX + 1))
                    for m in range(2):
                        for k in range(2):
                            last = pe.transpose(aux[:, k * NKF + m * P:k * NKF + (m + 1) * P],
                                                cx_in[j % NCTX][:, m, k * P:(k + 1) * P], ident[:])
                elif name[:2] == "LV":
                    n = int(name[2])
                    pe.wait_ge(left_ready, g + 1)
                    for k in range(2):
                        last = pe.matmul(aux[:], leftr[:, k].rearrange("p r b -> p (r b)"), wvn[:, k, n * 512:(n + 1) * 512],
                                         start=(k == 0), stop=(k == 1))
                else:
                    pe.wait_ge(lastp_ready, (g + 1) * GB)
                    last = pe.transpose(aux[0:NT * GB, 0:P], lastp[:].rearrange("p t b -> p (t b)"), ident[:])
                last.then_inc(aux_full, 1)

            def scores(g, j, t):
                n = j * NT + t
                if n == 0:
                    pe.wait_ge(qk_copied_act, (g + 1) * (NH // 2))
                    pe.wait_ge(qk_copied_dve, (g + 1) * (NH // 2))
                elif n >= 2:
                    pe.wait_ge(scores_masked, g * GB * NT + n - 1)
                if t == 0:
                    pe.wait_ge(aux_free, nth(AUX, f"CT{j}", g))
                    pe.wait_ge(col_ready, g * GB + j + 1)
                for k in range(2):
                    last = pe.matmul(score[t % 2][:, 0:NK], qk[:, k, j, t * P:(t + 1) * P], cT[j % 2][:, k, :],
                                     start=(k == 0), stop=(k == 1))
                last.then_inc(scores_done, 1)

            def prob_transposes(g, j, half):
                n = 2 * (g * GB + j) + half
                pe.wait_ge(probs_ready, n + 1)
                after(pe, probT_copied, n)
                for m in range(2):
                    for i in range(2):
                        last = pe.transpose(probT[:, m * 256 + i * P:m * 256 + (i + 1) * P],
                                            pr[j % 2][:, 2 * half + i, m * P:(m + 1) * P], ident[:])
                last.then_inc(probT_full, 1)

            def weigh(g, j):
                pe.wait_ge(probT_copied, 2 * (g * GB + j) + 2)
                after(pe, acm_copied, g * GB + j)
                after(pe, act_copied, g * GB + j)
                c = cx_in[j % NCTX]
                for m in range(2):
                    pe.matmul(ac_main[:], c[:, m, 0:P], prT[:, m, :], start=(m == 0), stop=(m == 1))
                    by_pair = prT[:, m, :].rearrange("p (n r q) -> p n r q", r=2, q=NQ)
                    for r in range(2):
                        last = pe.matmul(ac_tail[r * 64:r * 64 + 64, 0:TOK], c[:, m, P:DC], by_pair[:, :, r, :],
                                         start=(m == 0), stop=(m == 1))
                last.then_inc(ac_done, 1)

            def post_job(name, g):
                if name not in POST:
                    return
                after(pe, post_free, nth(POST, name, g) - 1)
                if name[:2] == "OT":
                    n = int(name[2])
                    if n == 0:
                        pe.wait_ge(acm_copied, (g + 1) * GB)
                        pe.wait_ge(act_copied, (g + 1) * GB)
                        pe.wait_ge(aux_free, (g + 1) * len(AUX))
                    for i in range(2):
                        p, half = 2 * n + i, slice(i * TOK, (i + 1) * TOK)
                        for r in range(2):
                            pe.matmul(post[r * 64:r * 64 + 64, half], wvn[:, 0, (2 * p + r) * DH:(2 * p + r + 1) * DH],
                                      acm[:, 2 * p + r, :], start=True, stop=False)
                        pe.matmul(post[:, half], wvb[:, p, :], act_[:, p, :], start=False, stop=False)
                        last = pe.matmul(post[:, half], lv[:, 2 * p:2 * p + 2, :].rearrange("p h d -> p (h d)"),
                                         spread[:].rearrange("p b q -> p (b q)"), start=False, stop=True)
                elif name[:2] == "WO":
                    a = int(name[2])
                    for k in range(NPAIR):
                        last = pe.matmul(post[:, 0:DM], qT[:, k, a * P:(a + 1) * P], wo[:, k, :],
                                         start=(k == 0), stop=(k == NPAIR - 1))
                elif name == "T2":
                    pe.wait_ge(ln_ready[1], g + 1)
                    last = transposes(post, hn)
                elif name in ("QT", "KT"):
                    for c in range(2):
                        w0 = (0 if name == "QT" else DM) + c * P
                        for k in range(2):
                            last = pe.matmul(post[:, c * TOK:(c + 1) * TOK], wqkv[:, k, w0:w0 + P], hT[:, k, :],
                                             start=(k == 0), stop=(k == 1))
                elif name[:2] == "SC":
                    a = int(name[2])
                    for c in range(2):
                        for b in range(4):
                            at = (a * 4 + b) * NQ
                            last = pe.matmul(post[b * NQ:(b + 1) * NQ, c * 256:(c + 1) * 256], q2T[:, c, at:at + NQ],
                                             kM[:, c, :, at:at + NQ], start=True, stop=True)
                elif name == "VR":
                    for k in range(2):
                        vw = wqkv[:, k, 2 * DM:3 * DM].rearrange("p (c r d) -> p c r d", c=4, r=4)
                        for b in range(GB):
                            for r in range(4):
                                last = pe.matmul(post[r * NQ:(r + 1) * NQ, b * 64:(b + 1) * 64], hT[:, k, b * NQ:(b + 1) * NQ],
                                                 vw[:, :, r, :], start=(k == 0 and b == 0), stop=(k == 1), skip_group_check=True)
                elif name[:2] == "PT":
                    a = int(name[2])
                    pe.wait_ge(p2_ready, 2 * g + a + 1)
                    flat = sc[:, a].rearrange("p h k -> p (h k)")
                    for c in range(4):
                        last = pe.transpose(post[:, c * P:(c + 1) * P], flat[:, c * P:(c + 1) * P], ident[:])
                elif name == "PV":
                    for a in range(2):
                        for c in range(4):
                            for b in range(4):
                                last = pe.matmul(post[b * NQ:(b + 1) * NQ, a * DM + c * 64:a * DM + (c + 1) * 64],
                                                 p2T[:, a, c, b * NQ:(b + 1) * NQ],
                                                 vb[:, a * 4 + b, c].rearrange("p r d -> p (r d)"), start=True, stop=True)
                elif name == "T4":
                    last = transposes(post, cv)
                elif name == "PJ":
                    for a in range(2):
                        for k in range(2):
                            last = pe.matmul(post[:, a * DM:(a + 1) * DM], cvT[:, k, a * P:(a + 1) * P], wproj[:, k, :],
                                             start=(k == 0), stop=(k == 1))
                elif name == "T3":
                    pe.wait_ge(ln_ready[2], g + 1)
                    last = transposes(post, hn)
                elif name == "FK":
                    pe.wait_ge(mixed, g + 1)
                    for m in range(2):
                        for k in range(2):
                            last = pe.matmul(post[:, m * TOK:(m + 1) * TOK], wkT[:, k, m * P:(m + 1) * P], mix[:, 2 + k, :],
                                             start=(k == 0), stop=(k == 1))
                elif name == "FR":
                    pe.wait_ge(mixed, g + 1)
                    for a in range(2):
                        for k in range(2):
                            last = pe.matmul(post[:, a * DM:(a + 1) * DM], mix[:, k, a * P:(a + 1) * P], wrT[:, k, :],
                                             start=(k == 0), stop=(k == 1))
                elif name == "FV":
                    pe.wait_ge(ka_ready, g + 1)
                    for a in range(2):
                        for k in range(2):
                            last = pe.matmul(post[:, a * DM:(a + 1) * DM], ka[:, k, a * P:(a + 1) * P], wvT[:, k, :],
                                             start=(k == 0), stop=(k == 1))
                last.then_inc(post_full, 1)

            def job(name, g):
                if name in PRE:
                    pre_job(name, g + 1)
                elif name in AUX:
                    aux_job(name, g)
                else:
                    post_job(name, g - 1)

            def group(g, has_pre, has_post):
                aux_job("CT0", g)
                for j in range(GB):
                    for piece in range(8):
                        if piece == 0 and j < GB - 1:
                            aux_job(f"CT{j + 1}", g)
                        elif piece in (1, 2):
                            scores(g, j, piece - 1)
                        elif piece in (4, 5):
                            scores(g, j, piece - 2)
                        elif piece in (3, 6) and j > 0:
                            prob_transposes(g, j - 1, piece // 3 - 1)
                        elif piece == 7 and j > 0:
                            weigh(g, j - 1)
                        for name in jobs_at(j, piece, has_pre, has_post):
                            job(name, g)
                for n in range(NH + 4):
                    if n == 2:
                        prob_transposes(g, GB - 1, 0)
                    if n == 5:
                        prob_transposes(g, GB - 1, 1)
                    if n == 8:
                        weigh(g, GB - 1)
                    if n == 9:
                        aux_job("LT", g)
                    if n < NH and has_pre:
                        qk_job(n, g + 1)

            for name in PRE:
                pre_job(name, 0)
            for h in range(NH):
                qk_job(h, 0)
            groups(pe, group)
            for name in POST:
                post_job(name, NG - 1)

        @block.scalar
        def _(act):
            act.wait_ge(zeroed, 4)
            act.wait_ge(setup_full, 1)
            act.activation(left[:, 0, :], banks[0][:, 0:NB], ACT.Copy)
            act.activation(left[0:64, 1, :], banks[0][0:64, NB:2 * NB], ACT.Copy).then_inc(setup_copied, 1)
            for n, w in enumerate((wrT, wkT, wvT)):
                act.wait_ge(setup_full, 6 + n)
                act.activation(w[:].rearrange("p k d -> p (k d)"), banks[5 + n][:], ACT.Copy).then_inc(setup_copied, 1)
            act.wait_ge(small_in, 16 * N_SMALL)

            def pre_job(name, g):
                act.wait_ge(pre_full, nth(PRE, name, g))
                if name == "XT":
                    for k in range(2):
                        last = act.activation(xnT[:, k, :], pre[:, k * TOK:(k + 1) * TOK], ACT.Identity,
                                              bias=cols[:, B1, k:k + 1], scale=cols[:, G1, k:k + 1])
                else:
                    n = int(name[1])
                    last = act.activation(qT[:, 2 * n:2 * n + 2, :].rearrange("p n t -> p (n t)"), pre[:], ACT.Copy)
                last.then_inc(pre_free, 1)

            def qk_copy(h, g):
                act.wait_ge(qk_full, g * NH + h + 1)
                act.activation(qk[:, :, :, h * NQ:(h + 1) * NQ],
                               score[0][:].rearrange("p (k b q) -> p k b q", k=2, q=NQ), ACT.Copy).then_inc(qk_copied_act, 1)

            def context(g, j):
                act.wait_ge(aux_full, nth(AUX, f"CT{j}", g))
                after(act, scores_done, g * GB * NT + (j - 1) * NT)
                act.activation(cT[j % 2][:, :, 0:NKF], aux[:].rearrange("p (k m) -> p k m", k=2), ACT.Copy).then_inc(aux_free, 1)

            def exponent(g, j, t):
                act.wait_ge(scores_masked, g * GB * NT + j * NT + t + 1)
                if t == 0:
                    after(act, probT_full, 2 * (g * GB + j - 1))
                    after(act, lastp_ready, g * GB + j - 1)
                act.activation(pr[j % 2][:, t, :], sm[:, t, :], ACT.Exp, bias=nmx[:, j % 2, t:t + 1], scale=-1.0,
                               accum_out=ssum[:, j % 2, t:t + 1]).then_inc(exp_done, 1)

            def prob_copy(g, j):
                act.wait_ge(probT_full, 2 * (g * GB + j) + 2)
                act.activation(prT[:, :, 256:512], probT[:].rearrange("p (m c) -> p m c", m=2), ACT.Copy).then_inc(probT_copied, 1)

            def weighed(g, j):
                act.wait_ge(ac_done, g * GB + j + 1)
                act.activation(acm[:, :, j * NQ:(j + 1) * NQ], ac_main[:].rearrange("p (h q) -> p h q", q=NQ),
                               ACT.Copy).then_inc(acm_copied, 1)

            def post_job(name, g):
                if name not in ("OT0", "OT2", "T2", "QT", "SC0", "SC1", "PT0", "PT1", "PV", "T4", "T3", "FK", "FR"):
                    return
                if name[:2] == "SC":
                    a = int(name[2])
                    act.wait_ge(post_free, nth(POST, name, g))
                    act.activation(sc[:, a], sc[:, a], ACT.Exp, scale=float(SD) ** -0.5).then_inc(sexp_done, 1)
                    return
                if name == "FR":
                    act.wait_ge(post_free, nth(POST, name, g))
                    act.activation(er[:], er[:], ACT.Exp, scale=-1.0).then_inc(er_exp, 1)
                    return
                act.wait_ge(post_full, nth(POST, name, g))
                if name[:2] == "OT":
                    n = int(name[2])
                    last = act.activation(qT[:, 2 * n:2 * n + 2, :].rearrange("p n t -> p (n t)"), post[:], ACT.Copy)
                elif name == "T2":
                    for k in range(2):
                        last = act.activation(hT[:, k, :], post[:, k * TOK:(k + 1) * TOK], ACT.Identity,
                                              bias=cols[:, B2, k:k + 1], scale=cols[:, G2, k:k + 1])
                elif name == "QT":
                    for k in range(2):
                        last = act.activation(q2T[:, k, :], post[:, k * TOK:(k + 1) * TOK], ACT.Identity, bias=bcol[:, k:k + 1])
                elif name[:2] == "PT":
                    last = act.activation(p2T[:, int(name[2])].rearrange("p c q -> p (c q)"), post[:], ACT.Copy)
                elif name == "PV":
                    last = act.activation(cv[:].rearrange("p a c -> p (a c)"), post[:], ACT.Copy)
                elif name == "T4":
                    for k in range(2):
                        last = act.activation(cvT[:, k, :], post[:, k * TOK:(k + 1) * TOK], ACT.Identity, bias=bcol[:, 4 + k:5 + k])
                elif name == "T3":
                    last = act.activation(x3T[:, :, :, 1:NQ + 1], post[:].rearrange("p (k b q) -> p k b q", k=2, q=NQ), ACT.Copy)
                elif name == "FK":
                    after(act, ka_ready, g)
                    last = act.activation(kr.rearrange("p k t -> p (k t)"), post[:], ACT.Relu)
                last.then_inc(post_free, 1)

            def job(name, g):
                if name in PRE:
                    pre_job(name, g + 1)
                elif name not in AUX:
                    post_job(name, g - 1)

            def group(g, has_pre, has_post):
                context(g, 0)
                for j in range(GB):
                    for piece in range(8):
                        if piece == 0 and j < GB - 1:
                            context(g, j + 1)
                        elif piece in (1, 2):
                            exponent(g, j, piece - 1)
                        elif piece in (4, 5):
                            exponent(g, j, piece - 2)
                        elif piece == 6 and j > 0:
                            prob_copy(g, j - 1)
                        elif piece == 7 and j > 0:
                            weighed(g, j - 1)
                        for name in jobs_at(j, piece, has_pre, has_post):
                            job(name, g)
                for n in range(NH + 4):
                    if n == 5:
                        prob_copy(g, GB - 1)
                    if n == 8:
                        weighed(g, GB - 1)
                    if n < NH and n % 2 == 0 and has_pre:
                        qk_copy(n, g + 1)

            for name in PRE:
                pre_job(name, 0)
            for h in range(0, NH, 2):
                qk_copy(h, 0)
            groups(act, group)
            for name in POST:
                post_job(name, NG - 1)

        @block.vector
        def _(dve):
            dve.wait_ge(ident_made, 2)
            dve.tensor_reduce(headm[:], ident[:].rearrange("p (h d) -> p h d", d=16), AX.X, ALU.add).then_inc(consts_made, 1)
            dve.tensor_reduce(seqm[:], ident[0:NQ, 0:NQ].rearrange("p (t b) -> p b t", b=GB), AX.X, ALU.add).then_inc(consts_made, 1)
            dve.tensor_reduce(leftm[:], ident[:].rearrange("p (r t b) -> p t r b", r=4, b=GB), AX.X, ALU.add).then_inc(consts_made, 1)
            dve.wait_ge(mask_in, 64)
            dve.tensor_reduce(poison[:, 1:2], mraw[:], AX.X, ALU.max).then_inc(consts_made, 1)
            dve.tensor_scalar(mbias[:], mraw[:], -MASKED, MASKED, ALU.mult, ALU.add).then_inc(consts_made, 1)
            dve.wait_ge(consts_made, 5)
            dve.reciprocal(poison[:, 0:1], poison[:, 1:2]).then_inc(consts_made, 1)
            dve.wait_ge(consts_made, 6)
            dve.tensor_tensor(poison[:, 0:1], poison[:, 0:1], poison[:, 1:2], ALU.mult).then_inc(setup_copied, 1)
            dve.wait_ge(zeroed, 3)
            for n in range(4):
                dve.wait_ge(setup_full, 2 + n)
                src = banks[1 + n][:, 0:2 * DC].rearrange("p (i c) -> p i c", i=2)
                for r in range(2):
                    half = slice(r * 64, r * 64 + 64)
                    dst = nwk[half, 0:NH * DC].rearrange("p (n r c) -> p n r c", r=2, c=DC)[:, 2 * n:2 * n + 2, r, :]
                    last = dve.tensor_scalar(dst, src[half], -1.0, None, ALU.mult)
                last.then_inc(setup_copied, 1)

            def layer_norm(n, g, src, dst, scale, shift):
                links = [0]

                def link(ins):
                    links[0] += 1
                    ins.then_inc(ln_link[n], 1)
                    dve.wait_ge(ln_link[n], g * LN_LINKS + links[0])

                w, y, q = lw[:, n, 0, :], lw[:, n, 1, :], lw[:, n, 2, :]
                dve.bn_stats(st[:, n, 0, :], src[:, 0, :])
                link(dve.bn_stats(st[:, n, 1, :], src[:, 1, :]))
                alone(dve)
                dve.bn_aggr(mv[:, n, 0, :], st[:, n, 0, :])
                link(dve.bn_aggr(mv[:, n, 1, :], st[:, n, 1, :]))
                link(dve.tensor_scalar(w, mv[:, n, :, 1], scale, shift, ALU.mult, ALU.add))
                link(dve.tensor_scalar(li[:, n, :], w.bitcast(I32), 1, None, ALU.logical_shift_right))
                link(dve.tensor_scalar(y.bitcast(I32), li[:, n, :], -1.0, RSQRT_SEED, ALU.mult, ALU.add))
                for _ in range(NEWTON):
                    link(dve.tensor_tensor(q, y, y, ALU.mult))
                    link(dve.scalar_tensor_tensor(out=q, in0=q, scalar=-0.5, in1=w, op0=ALU.mult, op1=ALU.mult))
                    link(dve.scalar_tensor_tensor(out=y, in0=q, scalar=1.5, in1=y, op0=ALU.add, op1=ALU.mult))
                assert links[0] == LN_LINKS
                for a in range(2):
                    last = dve.tensor_scalar(dst[:, a, :], src[:, a, :], mv[:, n, a, 0:1], y[:, a:a + 1],
                                             ALU.subtract, ALU.mult)
                last.then_inc(ln_ready[n], 1)

            def norm_input(g):
                dve.wait_ge(x_in, 16 * (g + 1))
                layer_norm(0, g, xn, xn, 1.0 + EPS, EPS * EPS)

            def qk_copy(h, g):
                dve.wait_ge(qk_full, g * NH + h + 1)
                dve.tensor_copy(qk[:, :, :, h * NQ:(h + 1) * NQ],
                                score[1][:].rearrange("p (k b q) -> p k b q", k=2, q=NQ)).then_inc(qk_copied_dve, 1)

            def mask_scores(g, j, t):
                n = g * GB * NT + j * NT + t
                dve.wait_ge(scores_done, n + 1)
                after(dve, exp_done, n - NT + 1)
                alone(dve)
                dve.tensor_tensor_reduce(sm[:, t, :], score[t % 2][:, 0:NK], mbias[:], DH ** -0.5, BIG,
                                         ALU.add, ALU.min, nmx[:, j % 2, t:t + 1]).then_inc(scores_masked, 1)

            def reciprocals(g, j, half):
                dve.wait_ge(exp_done, g * GB * NT + j * NT + 2 * half + 2)
                s = slice(2 * half, 2 * half + 2)
                dve.reciprocal(rsum[:, j % 2, s], ssum[:, j % 2, s]).then_inc(recip_done, 1)

            def prob_copy(g, j):
                dve.wait_ge(probT_full, 2 * (g * GB + j) + 1)
                after(dve, ac_done, g * GB + j)
                dve.tensor_copy(prT[:, :, 0:256], probT[:].rearrange("p (m c) -> p m c", m=2)).then_inc(probT_copied, 1)

            def weighed(g, j):
                dve.wait_ge(ac_done, g * GB + j + 1)
                dve.tensor_copy(act_[:, :, j * NQ:(j + 1) * NQ],
                                ac_tail[:, 0:TOK].rearrange("p (n q) -> p n q", q=NQ)).then_inc(act_copied, 1)

            def aux_job(name, g):
                if name[:2] == "LV":
                    n = int(name[2])
                    dve.wait_ge(aux_full, nth(AUX, name, g))
                    keep = leftm[:, 2 * n:2 * n + 2].rearrange("p t r -> p (t r)").unsqueeze(2).broadcast_to([P, 8, DH])
                    dve.tensor_tensor(lv[:, 8 * n:8 * n + 8, :], aux[:].rearrange("p (h d) -> p h d", d=DH), keep,
                                      ALU.mult).then_inc(aux_free, 1)
                elif name == "LT":
                    dve.wait_ge(aux_full, nth(AUX, name, g))
                    for r in range(4):
                        own = aux[0:NQ, r * NQ:(r + 1) * NQ].unsqueeze(1).broadcast_to([NQ, GB, NQ])
                        last = dve.tensor_tensor(spread[r * NQ:(r + 1) * NQ], own,
                                                 seqm[:].unsqueeze(2).broadcast_to([NQ, GB, NQ]), ALU.mult)
                    last.then_inc(aux_free, 1)

            def post_job(name, g):
                if name in ("OT1", "OT3"):
                    n = int(name[2])
                    dve.wait_ge(post_full, nth(POST, name, g))
                    dve.tensor_copy(qT[:, 2 * n:2 * n + 2, :].rearrange("p n t -> p (n t)"), post[:]).then_inc(post_free, 1)
                elif name in ("WO0", "WO1"):
                    a = int(name[2])
                    dve.wait_ge(post_full, nth(POST, name, g))
                    dve.wait_ge(xb_ready, g + 1)
                    after(dve, y_ready, g)
                    dve.tensor_tensor(x1[:, a, :], post[:, 0:DM], xb[:, a, :], ALU.add).then_inc(post_free, 1)
                    if a == 1:
                        dve.wait_ge(post_free, nth(POST, name, g))
                        layer_norm(1, g, x1, hn, 1.0 + EPS, EPS * EPS)
                elif name == "KT":
                    dve.wait_ge(post_full, nth(POST, name, g))
                    for c in range(2):
                        last = dve.scalar_tensor_tensor(
                            out=kM[:, c], in0=post[:, c * TOK:(c + 1) * TOK].unsqueeze(1).broadcast_to([P, 8, TOK]),
                            scalar=bcol[:, 2 + c:3 + c], in1=headm[:].unsqueeze(2).broadcast_to([P, 8, TOK]),
                            op0=ALU.add, op1=ALU.mult)
                    last.then_inc(post_free, 1)
                elif name[:2] == "SC":
                    a = int(name[2])
                    dve.wait_ge(post_full, nth(POST, name, g))
                    rows = post[:].rearrange("p (h k) -> p h k", k=NQ)
                    dve.tensor_reduce(smx[:, a, :], rows, AX.X, ALU.max).then_inc(smx_ready, 1)
                    dve.wait_ge(smx_ready, 2 * g + a + 1)
                    dve.tensor_tensor(sc[:, a], rows, smx[:, a, :].unsqueeze(2).broadcast_to([P, SH, NQ]),
                                      ALU.subtract).then_inc(post_free, 1)
                elif name[:2] == "SM":
                    a = int(name[2])
                    dve.wait_ge(sexp_done, 2 * g + a + 1)
                    dve.tensor_reduce(ssm[:, a, :], sc[:, a], AX.X, ALU.add).then_inc(ssum_done, 1)
                    dve.wait_ge(ssum_done, 4 * g + 2 * a + 1)
                    dve.tensor_scalar(ssm[:, a, :], ssm[:, a, :], 1e-12, None, ALU.max).then_inc(ssum_done, 1)
                    dve.wait_ge(ssum_done, 4 * g + 2 * a + 2)
                    dve.reciprocal(rs2[:, a, :], ssm[:, a, :]).then_inc(srecip_done, 1)
                elif name == "VR":
                    dve.wait_ge(post_full, nth(POST, name, g))
                    for r in range(4):
                        rows = slice(r * NQ, (r + 1) * NQ)
                        last = dve.tensor_copy(vb[rows, :, :, r, :],
                                               post[rows].rearrange("p (b c d) -> p b c d", b=GB, c=4))
                    last.then_inc(post_free, 1)
                elif name == "PJ":
                    dve.wait_ge(post_full, nth(POST, name, g))
                    dve.wait_ge(x1b_ready, g + 1)
                    dve.tensor_tensor(x2[:].rearrange("p a c -> p (a c)"), post[:], xb[:].rearrange("p a c -> p (a c)"),
                                      ALU.add).then_inc(post_free, 1)
                    dve.wait_ge(post_free, nth(POST, name, g))
                    layer_norm(2, g, x2, hn, 1.0, EPS)
                elif name == "MIX":
                    dve.wait_ge(post_free, nth(POST, "T3", g))
                    for s, (mu, mu1) in enumerate(((MUR, MUR1), (MUK, MUK1))):
                        for k in range(2):
                            last = dve.tensor_scalar(mixt[:, 2 * s + k, :].rearrange("p (b q) -> p b q", q=NQ),
                                                     x3T[:, k, :, 0:NQ], cols[:, mu1, k:k + 1], None, ALU.mult)
                    last.then_inc(half_mixed, 1)
                    dve.wait_ge(half_mixed, g + 1)
                    for s, (mu, mu1) in enumerate(((MUR, MUR1), (MUK, MUK1))):
                        for k in range(2):
                            last = dve.scalar_tensor_tensor(out=mix[:, 2 * s + k, :].rearrange("p (b q) -> p b q", q=NQ),
                                                            in0=x3T[:, k, :, 1:NQ + 1], scalar=cols[:, mu, k:k + 1],
                                                            in1=mixt[:, 2 * s + k, :].rearrange("p (b q) -> p b q", q=NQ),
                                                            op0=ALU.mult, op1=ALU.add)
                    last.then_inc(mixed, 1)
                elif name == "FR":
                    dve.wait_ge(post_full, nth(POST, name, g))
                    after(dve, y_ready, g)
                    dve.tensor_scalar(er[:].rearrange("p a c -> p (a c)"), post[:], EXP_MAX, None, ALU.max).then_inc(post_free, 1)
                elif name == "SG":
                    dve.wait_ge(er_exp, g + 1)
                    dve.tensor_scalar(er[:], er[:], 1.0, None, ALU.add).then_inc(er_one, 1)
                    dve.wait_ge(er_one, g + 1)
                    dve.reciprocal(er[:], er[:]).then_inc(r_ready, 1)
                elif name == "FV":
                    dve.wait_ge(post_full, nth(POST, name, g))
                    dve.wait_ge(r_ready, g + 1)
                    dve.tensor_tensor(er[:].rearrange("p a c -> p (a c)"), post[:], er[:].rearrange("p a c -> p (a c)"),
                                      ALU.mult).then_inc(post_free, 1)

            def job(name, g):
                if name == "LN1":
                    norm_input(g + 1)
                elif name in AUX:
                    aux_job(name, g)
                elif name not in PRE:
                    post_job(name, g - 1)

            def group(g, has_pre, has_post):
                for j in range(GB):
                    for piece in range(8):
                        if piece in (1, 2):
                            mask_scores(g, j, piece - 1)
                        elif piece in (4, 5):
                            mask_scores(g, j, piece - 2)
                        elif piece == 3 and j > 0:
                            prob_copy(g, j - 1)
                        elif piece == 7 and j > 0:
                            weighed(g, j - 1)
                        if piece == 1 and j > 0:
                            reciprocals(g, j - 1, 1)
                        if piece == 4:
                            reciprocals(g, j, 0)
                        for name in jobs_at(j, piece, has_pre, has_post):
                            job(name, g)
                reciprocals(g, GB - 1, 1)
                for n in range(NH + 4):
                    if n == 2:
                        prob_copy(g, GB - 1)
                    if n == 8:
                        weighed(g, GB - 1)
                    if n == 9:
                        aux_job("LT", g)
                    if n < NH and n % 2 == 1 and has_pre:
                        qk_copy(n, g + 1)

            dve.wait_ge(small_in, 16 * N_SMALL)
            dve.tensor_scalar(cols[:, MUR1:MUK1 + 1, :], cols[:, MUR:MUK + 1, :], -1.0, 1.0, ALU.mult, ALU.add).then_inc(consts_made, 1)
            dve.wait_ge(consts_made, 7)
            norm_input(0)
            for h in range(1, NH, 2):
                qk_copy(h, 0)
            groups(dve, group)
            for j in range(GB):
                for piece in range(8):
                    for name in jobs_at(j, piece, False, True):
                        if name not in AUX:
                            post_job(name, NG - 1)


_INS = ["x", "ctx_768", "mask_1x1xSxS2_bk0", "L0_xattn_ln_gamma", "L0_xattn_ln_beta", "L0_xattn_Wq", "L0_xattn_Wkv",
        "L0_xattn_Wo", "L0_xattn_bo", "L0_attn_ln_gamma", "L0_attn_ln_beta", "L0_attn_W_qkv", "L0_attn_b_qkv",
        "L0_attn_W_proj", "L0_attn_b_proj", "L0_ffn_W_r", "L0_ffn_W_k", "L0_ffn_W_v", "L0_ffn_mu_r", "L0_ffn_mu_k"]
_OUTS = [((NB, NQ, DM), "float32")]


def kernel(**inputs):
    import numpy as _np
    import concourse.bacc as _bacc
    from concourse import mybir as _mybir
    from concourse.bass_utils import run_bass_kernel_spmd as _run

    nc = _bacc.Bacc("TRN2", target_bir_lowering=False, num_devices=1)
    arrays, args = {}, []
    for name in _INS:
        a = _np.ascontiguousarray(inputs[name])
        arrays[f"in_{name}_dram"] = a
        args.append(nc.dram_tensor(f"in_{name}_dram", a.shape, _mybir.dt.from_np(a.dtype), kind="ExternalInput").ap())
    for i, (shape, dtype) in enumerate(_OUTS):
        dt = _mybir.dt.from_np(_np.dtype(dtype))
        args.append(nc.dram_tensor(f"out_{i}_dram", shape, dt, kind="ExternalOutput").ap())
    perceiver_layer(nc, *args)
    r = _run(nc, [arrays], core_ids=[0])
    return r.results[0]["out_0_dram"]
```

```python
from contextlib import ExitStack

import concourse.bass as bass
from concourse import mybir

ALU = mybir.AluOpType
ACT = mybir.ActivationFunctionType
AX = mybir.AxisListType
F32 = mybir.dt.float32
F32R = mybir.dt.float32r
I32 = mybir.dt.int32
U8 = mybir.dt.uint8

P = 128
NB, NQ, DM = 64, 32, 256
NK, DC = 257, 192
NKF = 256
NH, DH = 16, 64
SH, SD = 16, 16
GB = 8
NG = NB // GB
TOK = GB * NQ
XT_TILES = TOK // P
HT = 4
NT = NH // HT
NPAIR = NH // 2
NCTX = 4
EPS = 1e-5
BIG = 3.0e38
MASKED = 1.0e30
EXP_MAX = -87.0
RSQRT_SEED = float(0x5F3759DF)
NEWTON = 3

QK = [job for p in range(0, NPAIR, 2) for job in (("main", p), ("main", p + 1), ("tail", p))]
STEPS = [
    "R1 OT0 XB S0 N1 P0 CT OT1 A0 S1 S2 R0 A1 P1 OT2 S3 OT3 N0 AC A2".split(),
    "A3 R1 CT N1 S0 WO0 P0 S1 A4 R0 WO1 N0 B0 P1 S2 B1 S3 AC B2 B3".split(),
    "CT B4 S0 R1 N1 P0 T2 XT S1 S2 QT P1 Q0 R0 S3 N0 KT AC KM0".split(),
    "X1 KM1 S0 R1 VR N1 CT P0 S1 SC0 KM2 P1 KM3 E0 R0 N0 S2 SM0 S3 AC SC1 E1".split(),
    "W0 R1 N1 Q1 S0 SM1 PT0 P0 Q2 S1 S2 W1 R0 P1 CT PT1 S3 Q3 AC N0".split(),
    "R1 PV N1 P0 CT T4 S0 S1 S2 R0 PJ P1 C0 S3 C1 N0 C2 C3 AC".split(),
    "C4 CT T3 M0 S0 R1 M1 N1 S1 P0 LV0 S2 R0 FR N0 EZ P1 SG S3 FK AC".split(),
    "R1 N1 S0 P0 LV1 KA P1 S1 FV R0 N0 S2 S3 YO AC".split(),
    "R1 K0 K1 N1 P0 K2 K3 K4 P1 K5 K6 AC LT K7 K8 CT K9 K10 K11".split(),
]
FLOW = [name for step in STEPS for name in step]
AUX = ["CT0"]
for j, step in enumerate(STEPS[:GB]):
    AUX += [f"CT{j + 1}" if name == "CT" else name for name in step if name in ("CT", "LV0", "LV1")]
AUX.append("LT")
PRE = [name for name in FLOW if name in ("XT", "Q0", "Q1", "Q2", "Q3")]
POST = [name for name in FLOW if name in (
    "OT0", "OT1", "OT2", "OT3", "WO0", "WO1", "T2", "QT", "KT", "VR", "SC0", "SC1", "PT0", "PT1", "PV", "T4",
    "PJ", "T3", "FR", "FK", "FV")]
FOR_PRE = PRE + ["A0", "A1", "A2", "A3", "A4"] + [f"K{n}" for n in range(len(QK))]
CORE = ("CT", "S0", "S1", "S2", "S3", "R0", "R1", "N0", "N1", "P0", "P1", "AC", "LV0", "LV1", "LT")
ON_DVE = ("OT3", "P0",)
LN_LINKS = 5 + 3 * NEWTON


def perceiver_layer(nc, x, ctx_in, mask, g1, be1, Wq, Wkv, Wo, bo, g2, be2, Wqkv, bqkv, Wproj, bproj,
                    Wr, Wk, Wv, mur, muk, out):
    with ExitStack() as es:
        def sb(name, shape, dt=F32):
            return es.enter_context(nc.sbuf_tensor(name, shape, dt))

        def sem(name):
            return es.enter_context(nc.semaphore(name))

        def psum(name):
            return es.enter_context(nc.psum_tensor(name, [P, 512], F32))

        wq = sb("wq", [P, 2, NH * DH])
        nwk = sb("nwk", [P, NH, P])
        nwkt = sb("nwkt", [P, NPAIR, P])
        wvn = sb("wvn", [P, NH * DH])
        wvb = sb("wvb", [P, NPAIR, P])
        wo = sb("wo", [P, NPAIR, DM])
        wqkv = sb("wqkv", [P, 2, 3 * DM])
        wproj = sb("wproj", [P, 2, DM])
        wrT = sb("wrT", [P, 2, DM])
        wkT = sb("wkT", [P, 2, DM])
        wvT = sb("wvT", [P, 2, DM])
        cols = sb("cols", [P, 8, 2])
        G1, B1, G2, B2, MUR, MUK, MUR1, MUK1 = range(8)
        bcol = sb("bcol", [P, 6])
        bo_row = sb("bo_row", [P, DM])
        bp_row = sb("bp_row", [P, DM])
        ident = sb("ident", [P, P])
        mraw = sb("mraw", [P, NK], U8)
        mbias = sb("mbias", [P, NK])
        poison = sb("poison", [P, 2])
        headm = sb("headm", [P, 8])
        seqm = sb("seqm", [NQ, GB])
        leftm = sb("leftm", [P, 4, 4])
        left = sb("left", [P, 2, NB])
        left_h = sb("left_h", [P, 2, NB], F32R)
        left_l = sb("left_l", [P, 2, NB], F32R)
        leftr = sb("leftr", [P, 2, 16, GB])
        cx_in = [sb(f"cx_in{r}", [P, 2, 256]) for r in range(NCTX)]
        cT_h = [sb(f"cT_h{r}", [P, 2, NK + 1], F32R) for r in range(2)]
        cT_l = [sb(f"cT_l{r}", [P, 2, NK + 1], F32R) for r in range(2)]
        qk_h = sb("qk_h", [P, GB, NH * NQ], F32R)
        qk_l = sb("qk_l", [P, GB, NH * NQ], F32R)
        qk_t = sb("qk_t", [P, GB, NH * NQ], F32R)
        sm = sb("sm", [P, 2, NK])
        nmx = sb("nmx", [P, 2, NT])
        ssum = sb("ssum", [P, 2, NT])
        rsum = sb("rsum", [P, 2, NT])
        pr = [sb(f"pr{r}", [P, NT, NK]) for r in range(2)]
        prT = sb("prT", [P, 2, NH * NQ])
        lastp = sb("lastp", [P, NT, GB])
        spread = sb("spread", [P, GB, NQ])
        lv = sb("lv", [P, NH, DH])
        acm = sb("acm", [P, NH, TOK])
        act_ = sb("act_", [P, NPAIR, TOK])
        xn = sb("xn", [P, 2, DM])
        xnT = sb("xnT", [P, 2, TOK])
        qT = sb("qT", [P, NPAIR, TOK])
        xb = sb("xb", [P, 2, DM])
        x1 = sb("x1", [P, 2, DM])
        x2 = x1
        hn = sb("hn", [P, 2, DM])
        hT = sb("hT", [P, 2, TOK])
        q2T = sb("q2T", [P, 2, TOK])
        kT2 = hn
        kM = sb("kM", [P, 2, 8, P])
        sc = sb("sc", [P, 2, SH, NQ])
        smx = sb("smx", [P, 2, SH])
        ssm = sb("ssm", [P, 2, SH])
        rs2 = sb("rs2", [P, 2, SH])
        vb = sb("vb", [P, GB, 4, 4, SD])
        cv, cvT = hT, q2T
        x3T = sb("x3T", [P, 2, GB, NQ + 1])
        er = sc[:, 0].rearrange("p h k -> p (h k)").rearrange("p (a c) -> p a c", a=2)
        yo = sb("yo", [P, 2, DM])
        st = sb("st", [P, 3, 2, 6])
        mv = sb("mv", [P, 3, 2, 2])
        lw = sb("lw", [P, 3, 4, 2])
        li = sb("li", [P, 3, 2], I32)

        stage = acm[:].rearrange("p h t -> p (h t)")
        wk_main, wk_tail = stage[:, 0:1024], stage[0:64, 1024:2048]
        spare = kM[:].rearrange("p a b c -> p (a b c)")
        p2T = spare[:, 0:1024].rearrange("p (a c q) -> p a c q", a=2, c=4)
        mixt = spare[:, 0:1024].rearrange("p (s t) -> p s t", s=4)
        mix = spare[:, 1024:2048].rearrange("p (s t) -> p s t", s=4)
        kr = spare[:, 0:512].rearrange("p (k t) -> p k t", k=2)
        ka = spare[:, 512:1024].rearrange("p (k t) -> p k t", k=2)
        ffn_in = [stage[:, 2048 + 512 * n:2560 + 512 * n].rearrange("p (k c) -> p k c", k=2) for n in range(3)]
        left_in = stage[0:NB, 3584:3584 + 256]

        score = [psum("score0"), psum("score1")]
        probT, ac_main, ac_tail, aux, pre, post = (psum(n) for n in ("probT", "ac_main", "ac_tail", "aux", "pre", "post"))
        qk_bank = [score[0], score[1], pre]
        banks = [score[0], score[1], probT, ac_main, ac_tail, aux, pre, post]

        consts_made, ident_made, zeroed = sem("consts_made"), sem("ident_made"), sem("zeroed")
        weights_in, staged_in, mask_in, small_in = sem("weights_in"), sem("staged_in"), sem("mask_in"), sem("small_in")
        setup_full, setup_copied, left_upper = sem("setup_full"), sem("setup_copied"), sem("left_upper")
        waits_passed = sem("waits_passed")
        x_in, xres_in, stored = sem("x_in"), sem("xres_in"), sem("stored")
        ctx_loaded = [sem(f"ctx_loaded{r}") for r in range(NCTX)]
        left_ready, col_ready = sem("left_ready"), sem("col_ready")
        aux_full, aux_free = sem("aux_full"), sem("aux_free")
        pre_full, pre_free = sem("pre_full"), sem("pre_free")
        post_full, post_free = sem("post_full"), sem("post_free")
        qk_full, qk_upper, qk_split, ctx_upper, kM_ready = (sem(n) for n in ("qk_full", "qk_upper", "qk_split", "ctx_upper", "kM_ready"))
        scores_done, scores_masked, exp_done = sem("scores_done"), sem("scores_masked"), sem("exp_done")
        recip_done, probs_ready, lastp_ready = sem("recip_done"), sem("probs_ready"), sem("lastp_ready")
        probT_full, probT_copied = sem("probT_full"), sem("probT_copied")
        ac_done, acm_copied, act_copied = sem("ac_done"), sem("acm_copied"), sem("act_copied")
        ln_link = [sem(f"ln_link{n}") for n in range(3)]
        ln_ready = [sem(f"ln_ready{n}") for n in range(3)]
        xb_ready, x1b_ready, smx_ready = sem("xb_ready"), sem("x1b_ready"), sem("smx_ready")
        sexp_done, ssum_done, srecip_done, p2_ready = sem("sexp_done"), sem("ssum_done"), sem("srecip_done"), sem("p2_ready")
        half_mixed, mixed = sem("half_mixed"), sem("mixed")
        ka_ready, er_exp, er_one, r_ready = sem("ka_ready"), sem("er_exp"), sem("er_one"), sem("r_ready")
        y_ready = sem("y_ready")

        x_rows = x.rearrange("b n c -> (b n) c")
        out_rows = out.rearrange("b n c -> (b n) c")

        def token_rows(t, g):
            return t[bass.ds(g * TOK, TOK), :].rearrange("(a p) c -> p a c", p=P)

        def after(eng, s, value):
            if isinstance(value, int) and value <= 0:
                return
            eng.wait_ge(s, value)

        def alone(eng):
            eng.sem_inc(waits_passed)

        def nth(jobs, name, g):
            return g * len(jobs) + jobs.index(name) + 1

        def groups(eng, group):
            group(0, True, False)
            group(1, True, True)
            with eng.Fori(2, NG - 1) as g:
                group(g, True, True)
            group(NG - 1, False, True)

        def group_jobs(g, has_pre, has_post):
            for j, step in enumerate(STEPS):
                for name in step:
                    if name in CORE:
                        if not (j == 0 and name in ("R1", "N1", "P0", "P1", "AC")) and not (j == GB and name == "CT" and not has_pre):
                            yield j, name, g
                    elif name in FOR_PRE:
                        if has_pre:
                            yield j, name, g + 1
                    elif has_post:
                        yield j, name, g - 1

        def next_sequence(g, j):
            return g * GB + j + 1 if j < GB else (g + 1) * GB

        def next_context(g, j):
            return (f"CT{j + 1}", g) if j < GB - 1 else ("CT0", g + 1)

        def closing_jobs():
            for name in FLOW:
                if name not in CORE and name not in FOR_PRE:
                    yield name

        es.enter_context(nc.allow_non_contiguous_dma(reason="per-channel vectors, one element to a partition"))
        block = es.enter_context(nc.Block())

        N_WEIGHTS, N_STAGED, N_SMALL, N_SETUP, N_ZEROED = 7, 7, 9, 9, 5

        @block.sync
        def _(sp):
            def load_ctx(b, slot):
                rows = ctx_in[bass.ds(b, 1), 0:NKF, :].rearrange("o (k p) c -> p (o k) c", p=P)
                sp.dma_start(cx_in[slot][:, :, 0:DC], rows).then_inc(ctx_loaded[slot], 16)
                sp.dma_start(cx_in[slot][:, :, DC:256], rows[:, :, P:DC]).then_inc(ctx_loaded[slot], 16)

            def column(v):
                return v.rearrange("(k p) -> p k", p=P)

            sp.dma_start(xn[:], token_rows(x_rows, 0)).then_inc(x_in, 16)
            sp.dma_start(wk_main, Wkv[0:P, 0:NH * DH]).then_inc(staged_in, 16)
            sp.dma_start(wk_tail, Wkv[P:DC, 0:NH * DH]).then_inc(staged_in, 16)
            sp.dma_start(left_in[:, 0:DC], ctx_in[:, NKF, :]).then_inc(staged_in, 16)
            sp.dma_start(left_in[:, DC:256], ctx_in[:, NKF, P:DC]).then_inc(staged_in, 16)
            for n, w in enumerate((Wr, Wk, Wv)):
                sp.dma_start(ffn_in[n], w.rearrange("(k p) c -> p k c", p=P)).then_inc(staged_in, 16)
            for n, v in ((G1, g1), (B1, be1), (G2, g2), (B2, be2), (MUR, mur), (MUK, muk)):
                sp.dma_start(cols[:, n, :], column(v)).then_inc(small_in, 16)
            sp.dma_start(bcol[:], column(bqkv)).then_inc(small_in, 16)
            sp.dma_start(wq[:], Wq.rearrange("(k p) n -> p k n", p=P)).then_inc(weights_in, 16)
            for r in range(4):
                sp.dma_start(mraw[r * NQ:(r + 1) * NQ, :], mask[0, 0, :, :]).then_inc(mask_in, 16)
            for r in range(NCTX):
                load_ctx(r, r)
            sp.wait_ge(zeroed, 1)
            wv_all = Wkv[:, NH * DH:2 * NH * DH]
            sp.dma_start(wvn[:], wv_all[0:P, :]).then_inc(weights_in, 16)
            tails = wv_all[P:DC, :].rearrange("c (n r d) -> c n r d", r=2, d=DH)
            for r in range(2):
                sp.dma_start(wvb[r * 64:r * 64 + 64, :, r * 64:r * 64 + 64], tails[:, :, r, :]).then_inc(small_in, 16)
            sp.dma_start(wo[:], Wo.rearrange("(k p) n -> p k n", p=P)).then_inc(weights_in, 16)
            sp.dma_start(wqkv[:], Wqkv.rearrange("(k p) n -> p k n", p=P)).then_inc(weights_in, 16)
            sp.dma_start(wproj[:], Wproj.rearrange("(k p) n -> p k n", p=P)).then_inc(weights_in, 16)
            sp.dma_start(bo_row[:], bo.partition_broadcast(P)).then_inc(weights_in, 16)
            sp.dma_start(bp_row[:], bproj.partition_broadcast(P)).then_inc(weights_in, 16)

            def store(g):
                sp.wait_ge(y_ready, g + 1)
                sp.dma_start(token_rows(out_rows, g), yo[:]).then_inc(stored, 16)

            def load_residual(g):
                after(sp, y_ready, g)
                sp.dma_start(xb[:], token_rows(x_rows, g)).then_inc(xres_in, 16)

            def group(g, has_pre, has_post):
                if has_pre:
                    sp.wait_ge(pre_full, nth(PRE, "XT", g))
                    sp.dma_start(xn[:], token_rows(x_rows, g + 1)).then_inc(x_in, 16)
                if has_post:
                    load_residual(g - 1)
                for j in range(GB if has_pre else GB - NCTX):
                    sp.wait_ge(ac_done, g * GB + j + 1)
                    load_ctx(g * GB + j + NCTX, j % NCTX)
                if has_post:
                    store(g - 1)

            groups(sp, group)
            load_residual(NG - 1)
            store(NG - 1)
            sp.wait_ge(stored, 16 * NG)

        @block.gpsimd
        def _(pool):
            pool.memset(ident[:], 0.0).then_inc(ident_made, 1)
            pool.memset(wvb[:], 0.0).then_inc(zeroed, 1)
            pool.memset(nwk[:], 0.0)
            pool.memset(nwkt[:], 0.0).then_inc(zeroed, 1)
            pool.wait_ge(ident_made, 1)
            pool.affine_select(out=ident[:], in_=ident[:], compare_op=ALU.not_equal, fill=1.0, base=0,
                               pattern=[[-1, P]], channel_multiplier=1).then_inc(ident_made, 1)
            for r in range(2):
                pool.memset(cT_h[r][:, :, NK].bitcast(F32), 0.0)
                last = pool.memset(cT_l[r][:, :, NK].bitcast(F32), 0.0)
            last.then_inc(zeroed, 1)
            pool.memset(vb[:], 0.0).then_inc(zeroed, 1)
            pool.memset(x3T[:, :, :, 0], 0.0).then_inc(zeroed, 1)

            def columns(b, name):
                after(pool, scores_done, (b - 1) * NT)
                alone(pool)
                r = int(name[2]) % 2
                pool.tensor_copy(cT_h[r][:, :, NKF], left_h[:, :, bass.ds(b, 1)].rearrange("p k o -> p (k o)"))
                pool.tensor_copy(cT_l[r][:, :, NKF], left_l[:, :, bass.ds(b, 1)].rearrange("p k o -> p (k o)")).then_inc(col_ready, 1)

            def normalise(g, j, half):
                pool.wait_ge(recip_done, 2 * (g * GB + j) + half + 1)
                alone(pool)
                for t in (2 * half, 2 * half + 1):
                    p = pr[j % 2][:, t, :]
                    last = pool.tensor_scalar(p, p, rsum[:, j % 2, t:t + 1], poison[:, 0:1], ALU.mult, ALU.mult)
                last.then_inc(probs_ready, 1)
                if half == 1:
                    if j == 0:
                        after(pool, aux_full, g * len(AUX))
                    pool.wait_ge(probs_ready, 2 * (g * GB + j) + 2)
                    alone(pool)
                    pool.tensor_copy(lastp[:, :, j], pr[j % 2][:, :, NKF]).then_inc(lastp_ready, 1)

            def job(name, g):
                if name == "XB":
                    pool.wait_ge(xres_in, 16 * (g + 1))
                    for a in range(2):
                        last = pool.tensor_tensor(xb[:, a, :], xb[:, a, :], bo_row[:], ALU.add)
                    last.then_inc(xb_ready, 1)
                elif name == "X1":
                    pool.wait_ge(post_free, nth(POST, "WO1", g))
                    for a in range(2):
                        last = pool.tensor_tensor(xb[:, a, :], x1[:, a, :], bp_row[:], ALU.add)
                    last.then_inc(x1b_ready, 1)
                elif name in ("W0", "W1"):
                    a = int(name[1])
                    pool.wait_ge(srecip_done, 2 * g + a + 1)
                    pool.tensor_tensor(sc[:, a], sc[:, a], rs2[:, a, :].unsqueeze(2).broadcast_to([P, SH, NQ]),
                                       ALU.mult).then_inc(p2_ready, 1)
                elif name == "KA":
                    pool.wait_ge(post_free, nth(POST, "FK", g))
                    pool.tensor_tensor(ka, kr, kr, ALU.mult).then_inc(ka_ready, 1)
                elif name == "YO":
                    pool.wait_ge(post_free, nth(POST, "FV", g))
                    after(pool, stored, 16 * g)
                    pool.tensor_tensor(yo[:], er, x2[:], ALU.add).then_inc(y_ready, 1)

            def group(g, has_pre, has_post):
                after(pool, aux_full, g * len(AUX))
                alone(pool)
                pool.tensor_copy(leftr[:], left[:, :, bass.ds(g * GB, GB)].unsqueeze(2).broadcast_to([P, 2, 16, GB])).then_inc(left_ready, 1)
                for j, name, own in group_jobs(g, has_pre, has_post):
                    if name == "CT":
                        columns(next_sequence(g, j), next_context(g, j)[0])
                    elif name in ("N0", "N1"):
                        half = int(name[1])
                        normalise(g, j - half, half)
                    else:
                        job(name, own)

            pool.wait_ge(setup_copied, N_SETUP)
            pool.wait_ge(consts_made, 7)
            pool.wait_ge(weights_in, 16 * N_WEIGHTS)
            columns(0, "CT0")
            groups(pool, group)
            for name in closing_jobs():
                job(name, NG - 1)

        @block.tensor
        def _(pe):
            pe.wait_ge(ident_made, 2)
            pe.wait_ge(staged_in, 16 * N_STAGED)
            pe.transpose(banks[0][:, 0:NB], left_in[:, 0:P], ident[0:NB, 0:NB])
            pe.transpose(banks[0][:, NB:2 * NB], left_in[:, P:256], ident[0:NB, 0:NB]).then_inc(setup_full, 1)
            for n in range(4):
                for i in range(2):
                    pair = slice((2 * n + i) * P, (2 * n + i + 1) * P)
                    pe.transpose(banks[1 + n][:, i * DC:i * DC + P], wk_main[:, pair], ident[:])
                    last = pe.transpose(banks[1 + n][:, i * DC + P:(i + 1) * DC], wk_tail[:, pair], ident[0:64, 0:64])
                last.then_inc(setup_full, 1)
            for n in range(3):
                for kd in range(2):
                    for kc in range(2):
                        last = pe.transpose(banks[5 + n][:, kc * DM + kd * P:kc * DM + (kd + 1) * P],
                                            ffn_in[n][:, kd, kc * P:(kc + 1) * P], ident[:])
                last.then_inc(setup_full, 1)
            pe.wait_ge(setup_copied, N_SETUP)
            pe.wait_ge(zeroed, N_ZEROED)
            pe.wait_ge(weights_in, 16 * N_WEIGHTS)
            pe.wait_ge(small_in, 16 * N_SMALL)

            def transposes(bank, src):
                for a in range(2):
                    for k in range(2):
                        last = pe.transpose(bank[:, k * TOK + a * P:k * TOK + (a + 1) * P], src[:, a, k * P:(k + 1) * P], ident[:])
                return last

            def pre_job(name, g):
                after(pe, pre_free, nth(PRE, name, g) - 1)
                if name == "XT":
                    after(pe, qk_split, g * len(QK))
                if name == "XT":
                    pe.wait_ge(ln_ready[0], g + 1)
                    last = transposes(pre, xn)
                else:
                    n = int(name[1])
                    for i in range(2):
                        for k in range(2):
                            last = pe.matmul(pre[:, i * TOK:(i + 1) * TOK], wq[:, k, (2 * n + i) * P:(2 * n + i + 1) * P],
                                             xnT[:, k, :], start=(k == 0), stop=(k == 1))
                last.then_inc(pre_full, 1)

            def qk_job(n, g):
                bank = qk_bank[n % 3]
                if n == 0:
                    after(pe, scores_masked, g * GB * NT)
                    pe.wait_ge(pre_free, nth(PRE, "Q3", g))
                if n >= 3:
                    pe.wait_ge(qk_split, g * len(QK) + n - 2)
                kind, p = QK[n]
                for i in range(2):
                    half = bank[:, i * TOK:(i + 1) * TOK]
                    if kind == "main":
                        last = pe.matmul(half, nwk[:, 2 * p + i, :], qT[:, p, :], start=True, stop=True)
                    else:
                        last = pe.matmul(half, nwkt[:, p + i, :], qT[:, p + i, :], start=True, stop=True)
                last.then_inc(qk_full, 1)

            def aux_job(name, g):
                after(pe, aux_free, nth(AUX, name, g) - 1)
                if name[:2] == "CT":
                    j = int(name[2])
                    pe.wait_ge(ctx_loaded[j % NCTX], g * 32 * (GB // NCTX) + 32 * (j // NCTX + 1))
                    for m in range(2):
                        for k in range(2):
                            last = pe.transpose(aux[:, k * NKF + m * P:k * NKF + (m + 1) * P],
                                                cx_in[j % NCTX][:, m, k * P:(k + 1) * P], ident[:])
                elif name[:2] == "LV":
                    n = int(name[2])
                    pe.wait_ge(left_ready, g + 1)
                    for k, w in enumerate((wvn[:], wvb[:].rearrange("p n c -> p (n c)"))):
                        last = pe.matmul(aux[:], leftr[:, k].rearrange("p r b -> p (r b)"), w[:, n * 512:(n + 1) * 512],
                                         start=(k == 0), stop=(k == 1))
                else:
                    pe.wait_ge(lastp_ready, (g + 1) * GB)
                    last = pe.transpose(aux[0:NT * GB, 0:P], lastp[:].rearrange("p t b -> p (t b)"), ident[:])
                last.then_inc(aux_full, 1)

            def scores(g, j, t):
                n = j * NT + t
                if n == 0:
                    pe.wait_ge(qk_split, (g + 1) * len(QK))
                elif n >= 2:
                    pe.wait_ge(scores_masked, g * GB * NT + n - 1)
                if t == 0:
                    pe.wait_ge(aux_free, nth(AUX, f"CT{j}", g))
                    pe.wait_ge(col_ready, g * GB + j + 1)
                tile = slice(t * P, (t + 1) * P)
                c_h, c_l = cT_h[j % 2], cT_l[j % 2]
                products = [(qk_h, c_h[:, 0]), (qk_h, c_l[:, 0]), (qk_l, c_h[:, 0]), (qk_t, c_h[:, 1]), (qk_t, c_l[:, 1])]
                for i, (q, c) in enumerate(products):
                    last = pe.matmul(score[t % 2][:, 0:NK + 1], q[:, j, tile], c, start=(i == 0), stop=(i == len(products) - 1))
                last.then_inc(scores_done, 1)

            def prob_transposes(g, j, half):
                n = 2 * (g * GB + j) + half
                pe.wait_ge(probs_ready, n + 1)
                after(pe, probT_copied, n)
                for m in range(2):
                    for i in range(2):
                        last = pe.transpose(probT[:, m * 256 + i * P:m * 256 + (i + 1) * P],
                                            pr[j % 2][:, 2 * half + i, m * P:(m + 1) * P], ident[:])
                last.then_inc(probT_full, 1)

            def weigh(g, j):
                pe.wait_ge(probT_copied, 2 * (g * GB + j) + 2)
                after(pe, acm_copied, g * GB + j)
                after(pe, act_copied, g * GB + j)
                c = cx_in[j % NCTX]
                for m in range(2):
                    pe.matmul(ac_main[:], c[:, m, 0:P], prT[:, m, :], start=(m == 0), stop=(m == 1))
                    by_pair = prT[:, m, :].rearrange("p (n r q) -> p n r q", r=2, q=NQ)
                    for r in range(2):
                        last = pe.matmul(ac_tail[r * 64:r * 64 + 64, 0:TOK], c[:, m, P:DC], by_pair[:, :, r, :],
                                         start=(m == 0), stop=(m == 1))
                last.then_inc(ac_done, 1)

            def post_job(name, g):
                if name not in POST:
                    return
                after(pe, post_free, nth(POST, name, g) - 1)
                if name[:2] == "SC":
                    pe.wait_ge(kM_ready, 4 * g + 2 * int(name[2]) + 2)
                if name[:2] == "OT":
                    n = int(name[2])
                    if n == 0:
                        pe.wait_ge(acm_copied, (g + 1) * GB)
                        pe.wait_ge(act_copied, (g + 1) * GB)
                        pe.wait_ge(aux_free, (g + 1) * len(AUX))
                    for i in range(2):
                        p, half = 2 * n + i, slice(i * TOK, (i + 1) * TOK)
                        for r in range(2):
                            pe.matmul(post[r * 64:r * 64 + 64, half], wvn[:, (2 * p + r) * DH:(2 * p + r + 1) * DH],
                                      acm[:, 2 * p + r, :], start=True, stop=False)
                        pe.matmul(post[:, half], wvb[:, p, :], act_[:, p, :], start=False, stop=False)
                        last = pe.matmul(post[:, half], lv[:, 2 * p:2 * p + 2, :].rearrange("p h d -> p (h d)"),
                                         spread[:].rearrange("p b q -> p (b q)"), start=False, stop=True)
                elif name[:2] == "WO":
                    a = int(name[2])
                    for k in range(NPAIR):
                        last = pe.matmul(post[:, 0:DM], qT[:, k, a * P:(a + 1) * P], wo[:, k, :],
                                         start=(k == 0), stop=(k == NPAIR - 1))
                elif name == "T2":
                    pe.wait_ge(ln_ready[1], g + 1)
                    last = transposes(post, hn)
                elif name in ("QT", "KT"):
                    for c in range(2):
                        w0 = (0 if name == "QT" else DM) + c * P
                        for k in range(2):
                            last = pe.matmul(post[:, c * TOK:(c + 1) * TOK], wqkv[:, k, w0:w0 + P], hT[:, k, :],
                                             start=(k == 0), stop=(k == 1))
                elif name[:2] == "SC":
                    a = int(name[2])
                    for c in range(2):
                        for b in range(4):
                            at = (a * 4 + b) * NQ
                            last = pe.matmul(post[b * NQ:(b + 1) * NQ, c * 256:(c + 1) * 256], q2T[:, c, at:at + NQ],
                                             kM[:, c, :, b * NQ:(b + 1) * NQ], start=True, stop=True)
                elif name == "VR":
                    for k in range(2):
                        vw = wqkv[:, k, 2 * DM:3 * DM].rearrange("p (c r d) -> p c r d", c=4, r=4)
                        for b in range(GB):
                            for r in range(4):
                                last = pe.matmul(post[r * NQ:(r + 1) * NQ, b * 64:(b + 1) * 64], hT[:, k, b * NQ:(b + 1) * NQ],
                                                 vw[:, :, r, :], start=(k == 0 and b == 0), stop=(k == 1), skip_group_check=True)
                elif name[:2] == "PT":
                    a = int(name[2])
                    pe.wait_ge(p2_ready, 2 * g + a + 1)
                    flat = sc[:, a].rearrange("p h k -> p (h k)")
                    for c in range(4):
                        last = pe.transpose(post[:, c * P:(c + 1) * P], flat[:, c * P:(c + 1) * P], ident[:])
                elif name == "PV":
                    for a in range(2):
                        for c in range(4):
                            for b in range(4):
                                last = pe.matmul(post[b * NQ:(b + 1) * NQ, a * DM + c * 64:a * DM + (c + 1) * 64],
                                                 p2T[:, a, c, b * NQ:(b + 1) * NQ],
                                                 vb[:, a * 4 + b, c].rearrange("p r d -> p (r d)"), start=True, stop=True)
                elif name == "T4":
                    last = transposes(post, cv)
                elif name == "PJ":
                    for a in range(2):
                        for k in range(2):
                            last = pe.matmul(post[:, a * DM:(a + 1) * DM], cvT[:, k, a * P:(a + 1) * P], wproj[:, k, :],
                                             start=(k == 0), stop=(k == 1))
                elif name == "T3":
                    pe.wait_ge(ln_ready[2], g + 1)
                    last = transposes(post, hn)
                elif name == "FK":
                    pe.wait_ge(mixed, g + 1)
                    for m in range(2):
                        for k in range(2):
                            last = pe.matmul(post[:, m * TOK:(m + 1) * TOK], wkT[:, k, m * P:(m + 1) * P], mix[:, 2 + k, :],
                                             start=(k == 0), stop=(k == 1))
                elif name == "FR":
                    pe.wait_ge(mixed, g + 1)
                    for a in range(2):
                        for k in range(2):
                            last = pe.matmul(post[:, a * DM:(a + 1) * DM], mix[:, k, a * P:(a + 1) * P], wrT[:, k, :],
                                             start=(k == 0), stop=(k == 1))
                elif name == "FV":
                    pe.wait_ge(ka_ready, g + 1)
                    for a in range(2):
                        for k in range(2):
                            last = pe.matmul(post[:, a * DM:(a + 1) * DM], ka[:, k, a * P:(a + 1) * P], wvT[:, k, :],
                                             start=(k == 0), stop=(k == 1))
                last.then_inc(post_full, 1)

            def group(g, has_pre, has_post):
                for j, name, own in group_jobs(g, has_pre, has_post):
                    if name == "CT":
                        aux_job(*next_context(g, j))
                    elif name in ("LV0", "LV1", "LT"):
                        aux_job(name, g)
                    elif name in ("S0", "S1", "S2", "S3"):
                        scores(g, j, int(name[1]))
                    elif name in ("P0", "P1"):
                        prob_transposes(g, j - 1, int(name[1]))
                    elif name == "AC":
                        weigh(g, j - 1)
                    elif name in PRE:
                        pre_job(name, own)
                    elif name[0] == "K" and name in FOR_PRE:
                        qk_job(int(name[1:]), own)
                    else:
                        post_job(name, own)

            for name in PRE:
                pre_job(name, 0)
            for n in range(len(QK)):
                qk_job(n, 0)
            aux_job("CT0", 0)
            groups(pe, group)
            for name in POST:
                post_job(name, NG - 1)

        @block.scalar
        def _(act):
            act.wait_ge(setup_full, 1)
            act.activation(left[:].rearrange("p k b -> p (k b)"), banks[0][:, 0:2 * NB], ACT.Copy)
            act.activation(left_h[:].rearrange("p k b -> p (k b)"), banks[0][:, 0:2 * NB], ACT.Copy).then_inc(left_upper, 1)
            for n, w in enumerate((wrT, wkT, wvT)):
                act.wait_ge(setup_full, 6 + n)
                act.activation(w[:].rearrange("p k d -> p (k d)"), banks[5 + n][:], ACT.Copy).then_inc(setup_copied, 1)
            act.wait_ge(small_in, 16 * N_SMALL)

            def pre_job(name, g):
                act.wait_ge(pre_full, nth(PRE, name, g))
                if name == "XT":
                    for k in range(2):
                        last = act.activation(xnT[:, k, :], pre[:, k * TOK:(k + 1) * TOK], ACT.Identity,
                                              bias=cols[:, B1, k:k + 1], scale=cols[:, G1, k:k + 1])
                else:
                    n = int(name[1])
                    last = act.activation(qT[:, 2 * n:2 * n + 2, :].rearrange("p n t -> p (n t)"), pre[:], ACT.Copy)
                last.then_inc(pre_free, 1)

            def qk_copy(n, g):
                act.wait_ge(qk_full, g * len(QK) + n + 1)
                kind, p = QK[n]
                src = qk_bank[n % 3][:].rearrange("p (i b q) -> p b i q", i=2, q=NQ)
                if kind == "main":
                    dst = qk_h[:, :, 2 * p * NQ:(2 * p + 2) * NQ].rearrange("p b (i q) -> p b i q", q=NQ)
                    act.activation(dst, src, ACT.Copy).then_inc(qk_upper, 1)
                else:
                    for r in range(2):
                        rows = slice(r * 64, r * 64 + 64)
                        dst = qk_t[rows, :, 2 * p * NQ:(2 * p + 4) * NQ].rearrange("p b (i r q) -> p b i r q", r=2, q=NQ)[:, :, :, r]
                        last = act.activation(dst, src[rows], ACT.Copy)
                    last.then_inc(qk_upper, 1)

            def context(b, name, g):
                act.wait_ge(aux_full, nth(AUX, name, g))
                after(act, scores_done, (b - 1) * NT)
                r = int(name[2]) % 2
                act.activation(cT_h[r][:, :, 0:NKF], aux[:].rearrange("p (k m) -> p k m", k=2), ACT.Copy).then_inc(ctx_upper, 1)

            def exponent(g, j, t):
                act.wait_ge(scores_masked, g * GB * NT + j * NT + t + 1)
                if t == 0:
                    after(act, probT_full, 2 * (g * GB + j - 1))
                    after(act, lastp_ready, g * GB + j - 1)
                act.activation(pr[j % 2][:, t, :], sm[:, t % 2, :], ACT.Exp, bias=nmx[:, j % 2, t:t + 1], scale=-1.0,
                               accum_out=ssum[:, j % 2, t:t + 1]).then_inc(exp_done, 1)

            def prob_copy(g, j, half):
                act.wait_ge(probT_full, 2 * (g * GB + j) + half + 1)
                if half == 0:
                    after(act, ac_done, g * GB + j)
                act.activation(prT[:, :, half * 256:(half + 1) * 256], probT[:].rearrange("p (m c) -> p m c", m=2),
                               ACT.Copy).then_inc(probT_copied, 1)

            def weighed(g, j):
                act.wait_ge(ac_done, g * GB + j + 1)
                act.activation(acm[:, :, j * NQ:(j + 1) * NQ], ac_main[:].rearrange("p (h q) -> p h q", q=NQ),
                               ACT.Copy).then_inc(acm_copied, 1)

            def post_job(name, g):
                if name in ON_DVE or name not in ("OT0", "OT1", "OT2", "OT3", "T2", "QT", "KT", "E0", "E1", "PT0", "PT1", "PV", "T4", "T3", "FK", "EZ"):
                    return
                if name in ("E0", "E1"):
                    a = int(name[1])
                    act.wait_ge(post_free, nth(POST, f"SC{a}", g))
                    act.activation(sc[:, a], sc[:, a], ACT.Exp, scale=float(SD) ** -0.5).then_inc(sexp_done, 1)
                    return
                if name == "EZ":
                    act.wait_ge(post_free, nth(POST, "FR", g))
                    act.activation(er, er, ACT.Exp, scale=-1.0).then_inc(er_exp, 1)
                    return
                act.wait_ge(post_full, nth(POST, name, g))
                if name[:2] == "OT":
                    n = int(name[2])
                    last = act.activation(qT[:, 2 * n:2 * n + 2, :].rearrange("p n t -> p (n t)"), post[:], ACT.Copy)
                elif name == "T2":
                    for k in range(2):
                        last = act.activation(hT[:, k, :], post[:, k * TOK:(k + 1) * TOK], ACT.Identity,
                                              bias=cols[:, B2, k:k + 1], scale=cols[:, G2, k:k + 1])
                elif name == "QT":
                    for k in range(2):
                        last = act.activation(q2T[:, k, :], post[:, k * TOK:(k + 1) * TOK], ACT.Identity, bias=bcol[:, k:k + 1])
                elif name == "KT":
                    for k in range(2):
                        last = act.activation(kT2[:, k, :], post[:, k * TOK:(k + 1) * TOK], ACT.Identity, bias=bcol[:, 2 + k:3 + k])
                elif name[:2] == "PT":
                    last = act.activation(p2T[:, int(name[2])].rearrange("p c q -> p (c q)"), post[:], ACT.Copy)
                elif name == "PV":
                    last = act.activation(cv[:].rearrange("p a c -> p (a c)"), post[:], ACT.Copy)
                elif name == "T4":
                    for k in range(2):
                        last = act.activation(cvT[:, k, :], post[:, k * TOK:(k + 1) * TOK], ACT.Identity, bias=bcol[:, 4 + k:5 + k])
                elif name == "T3":
                    last = act.activation(x3T[:, :, :, 1:NQ + 1], post[:].rearrange("p (k b q) -> p k b q", k=2, q=NQ), ACT.Copy)
                elif name == "FK":
                    after(act, ka_ready, g)
                    last = act.activation(kr.rearrange("p k t -> p (k t)"), post[:], ACT.Relu)
                last.then_inc(post_free, 1)

            def group(g, has_pre, has_post):
                for j, name, own in group_jobs(g, has_pre, has_post):
                    if name == "CT":
                        context(next_sequence(g, j), *next_context(g, j))
                    elif name in ("S0", "S1", "S2", "S3"):
                        exponent(g, j, int(name[1]))
                    elif name in ("P0", "P1"):
                        if name not in ON_DVE:
                            prob_copy(g, j - 1, int(name[1]))
                    elif name == "AC":
                        weighed(g, j - 1)
                    elif name in PRE:
                        pre_job(name, own)
                    elif name[0] == "K" and name in FOR_PRE:
                        qk_copy(int(name[1:]), own)
                    elif name not in CORE:
                        post_job(name, own)

            for name in PRE:
                pre_job(name, 0)
            for n in range(len(QK)):
                qk_copy(n, 0)
            context(0, "CT0", 0)
            groups(act, group)
            for name in closing_jobs():
                post_job(name, NG - 1)

        @block.vector
        def _(dve):
            dve.wait_ge(ident_made, 2)
            dve.tensor_reduce(headm[:], ident[:].rearrange("p (h d) -> p h d", d=16), AX.X, ALU.add).then_inc(consts_made, 1)
            dve.tensor_reduce(seqm[:], ident[0:NQ, 0:NQ].rearrange("p (t b) -> p b t", b=GB), AX.X, ALU.add).then_inc(consts_made, 1)
            dve.tensor_reduce(leftm[:], ident[:].rearrange("p (r t b) -> p t r b", r=4, b=GB), AX.X, ALU.add).then_inc(consts_made, 1)
            dve.wait_ge(mask_in, 64)
            dve.tensor_reduce(poison[:, 1:2], mraw[:], AX.X, ALU.max).then_inc(consts_made, 1)
            dve.tensor_scalar(mbias[:], mraw[:], -MASKED, MASKED, ALU.mult, ALU.add).then_inc(consts_made, 1)
            dve.wait_ge(consts_made, 5)
            dve.reciprocal(poison[:, 0:1], poison[:, 1:2]).then_inc(consts_made, 1)
            dve.wait_ge(consts_made, 6)
            dve.tensor_tensor(poison[:, 0:1], poison[:, 0:1], poison[:, 1:2], ALU.mult).then_inc(setup_copied, 1)
            dve.wait_ge(left_upper, 1)
            dve.tensor_tensor(left_l[:].rearrange("p k b -> p (k b)"), banks[0][:, 0:2 * NB],
                              left_h[:].rearrange("p k b -> p (k b)"), ALU.subtract).then_inc(setup_copied, 1)
            dve.wait_ge(zeroed, 2)
            for n in range(4):
                dve.wait_ge(setup_full, 2 + n)
                src = banks[1 + n][:, 0:2 * DC].rearrange("p (i c) -> p i c", i=2)
                for r in range(2):
                    half = slice(r * 64, r * 64 + 64)
                    dst = nwk[half].rearrange("p (n r) c -> p n r c", r=2)[:, 2 * n:2 * n + 2, r, :]
                    dve.tensor_scalar(dst, src[half, :, 0:P], -1.0, None, ALU.mult)
                    last = dve.tensor_scalar(nwkt[half, 2 * n:2 * n + 2, r * 64:r * 64 + 64], src[half, :, P:DC], -1.0, None, ALU.mult)
                last.then_inc(setup_copied, 1)

            def layer_norm(n, stage, g, src, dst, scale, shift):
                def linked(i):
                    dve.wait_ge(ln_link[n], g * LN_LINKS + i)

                w, y, q = lw[:, n, 0, :], lw[:, n, 1, :], lw[:, n, 2, :]
                if stage == 0:
                    dve.bn_stats(st[:, n, 0, :], src[:, 0, :])
                    dve.bn_stats(st[:, n, 1, :], src[:, 1, :]).then_inc(ln_link[n], 1)
                    linked(1)
                    alone(dve)
                    dve.bn_aggr(mv[:, n, 0, :], st[:, n, 0, :])
                    dve.bn_aggr(mv[:, n, 1, :], st[:, n, 1, :]).then_inc(ln_link[n], 1)
                elif stage < 4:
                    if stage == 1:
                        linked(2)
                        dve.tensor_scalar(w, mv[:, n, :, 1], scale, shift, ALU.mult, ALU.add).then_inc(ln_link[n], 1)
                        linked(3)
                        dve.tensor_scalar(li[:, n, :], w.bitcast(I32), 1, None, ALU.logical_shift_right).then_inc(ln_link[n], 1)
                        linked(4)
                        dve.tensor_scalar(y.bitcast(I32), li[:, n, :], -1.0, RSQRT_SEED, ALU.mult, ALU.add).then_inc(ln_link[n], 1)
                    i = 5 + 3 * (stage - 1)
                    linked(i)
                    dve.tensor_tensor(q, y, y, ALU.mult).then_inc(ln_link[n], 1)
                    linked(i + 1)
                    dve.scalar_tensor_tensor(out=q, in0=q, scalar=-0.5, in1=w, op0=ALU.mult, op1=ALU.mult).then_inc(ln_link[n], 1)
                    linked(i + 2)
                    dve.scalar_tensor_tensor(out=y, in0=q, scalar=1.5, in1=y, op0=ALU.add, op1=ALU.mult).then_inc(ln_link[n], 1)
                else:
                    linked(LN_LINKS)
                    for a in range(2):
                        last = dve.tensor_scalar(dst[:, a, :], src[:, a, :], mv[:, n, a, 0:1], y[:, a:a + 1],
                                                 ALU.subtract, ALU.mult)
                    last.then_inc(ln_ready[n], 1)

            def norm_input(stage, g):
                if stage == 0:
                    dve.wait_ge(x_in, 16 * (g + 1))
                layer_norm(0, stage, g, xn, xn, 1.0 + EPS, EPS * EPS)

            def qk_lower(n, g):
                dve.wait_ge(qk_upper, g * len(QK) + n + 1)
                kind, p = QK[n]
                src = qk_bank[n % 3][:].rearrange("p (i b q) -> p b i q", i=2, q=NQ)
                if kind == "main":
                    upper, dst = (t[:, :, 2 * p * NQ:(2 * p + 2) * NQ].rearrange("p b (i q) -> p b i q", q=NQ) for t in (qk_h, qk_l))
                    dve.tensor_tensor(dst, src, upper, ALU.subtract).then_inc(qk_split, 1)
                else:
                    heads = qk_t[:, :, 2 * p * NQ:(2 * p + 4) * NQ].rearrange("p b (i r q) -> p b i r q", r=2, q=NQ)
                    for r in range(2):
                        own, other = slice(r * 64, r * 64 + 64), slice(64 - r * 64, 128 - r * 64)
                        last = dve.tensor_tensor(heads[other, :, :, r], src[own], heads[own, :, :, r], ALU.subtract)
                    last.then_inc(qk_split, 1)

            def ctx_lower(b, name, g):
                dve.wait_ge(ctx_upper, b + 1)
                r = int(name[2]) % 2
                dve.tensor_tensor(cT_l[r][:, :, 0:NKF], aux[:].rearrange("p (k m) -> p k m", k=2),
                                  cT_h[r][:, :, 0:NKF], ALU.subtract).then_inc(aux_free, 1)

            def mask_scores(g, j, t):
                n = g * GB * NT + j * NT + t
                dve.wait_ge(scores_done, n + 1)
                after(dve, exp_done, n - 1)
                alone(dve)
                dve.tensor_tensor_reduce(sm[:, t % 2, :], score[t % 2][:, 0:NK], mbias[:], DH ** -0.5, BIG,
                                         ALU.add, ALU.min, nmx[:, j % 2, t:t + 1]).then_inc(scores_masked, 1)

            def reciprocals(g, j, half):
                dve.wait_ge(exp_done, g * GB * NT + j * NT + 2 * half + 2)
                s = slice(2 * half, 2 * half + 2)
                dve.reciprocal(rsum[:, j % 2, s], ssum[:, j % 2, s]).then_inc(recip_done, 1)

            def prob_copy(g, j, half):
                dve.wait_ge(probT_full, 2 * (g * GB + j) + half + 1)
                if half == 0:
                    after(dve, ac_done, g * GB + j)
                dve.tensor_copy(prT[:, :, half * 256:(half + 1) * 256], probT[:].rearrange("p (m c) -> p m c", m=2)).then_inc(probT_copied, 1)

            def weighed(g, j):
                dve.wait_ge(ac_done, g * GB + j + 1)
                dve.tensor_copy(act_[:, :, j * NQ:(j + 1) * NQ],
                                ac_tail[:, 0:TOK].rearrange("p (n q) -> p n q", q=NQ)).then_inc(act_copied, 1)

            def aux_job(name, g):
                if name[:2] == "LV":
                    n = int(name[2])
                    dve.wait_ge(aux_full, nth(AUX, name, g))
                    keep = leftm[:, 2 * n:2 * n + 2].rearrange("p t r -> p (t r)").unsqueeze(2).broadcast_to([P, 8, DH])
                    dve.tensor_tensor(lv[:, 8 * n:8 * n + 8, :], aux[:].rearrange("p (h d) -> p h d", d=DH), keep,
                                      ALU.mult).then_inc(aux_free, 1)
                elif name == "LT":
                    dve.wait_ge(aux_full, nth(AUX, name, g))
                    for r in range(4):
                        own = aux[0:NQ, r * NQ:(r + 1) * NQ].unsqueeze(1).broadcast_to([NQ, GB, NQ])
                        last = dve.tensor_tensor(spread[r * NQ:(r + 1) * NQ], own,
                                                 seqm[:].unsqueeze(2).broadcast_to([NQ, GB, NQ]), ALU.mult)
                    last.then_inc(aux_free, 1)

            def post_job(name, g):
                if name[:2] == "OT" and name in ON_DVE:
                    n = int(name[2])
                    dve.wait_ge(post_full, nth(POST, name, g))
                    dve.tensor_copy(qT[:, 2 * n:2 * n + 2, :].rearrange("p n t -> p (n t)"), post[:]).then_inc(post_free, 1)
                elif name in ("WO0", "WO1"):
                    a = int(name[2])
                    dve.wait_ge(post_full, nth(POST, name, g))
                    dve.wait_ge(xb_ready, g + 1)
                    after(dve, y_ready, g)
                    dve.tensor_tensor(x1[:, a, :], post[:, 0:DM], xb[:, a, :], ALU.add).then_inc(post_free, 1)
                elif name[0] == "B":
                    if name == "B0":
                        dve.wait_ge(post_free, nth(POST, "WO1", g))
                    layer_norm(1, int(name[1]), g, x1, hn, 1.0 + EPS, EPS * EPS)
                elif name[:2] == "KM":
                    a, c = divmod(int(name[2]), 2)
                    if name == "KM0":
                        dve.wait_ge(post_free, nth(POST, "KT", g))
                    if name == "KM2":
                        dve.wait_ge(post_full, nth(POST, "SC0", g))
                    dve.tensor_tensor(kM[:, c], kT2[:, c, a * P:(a + 1) * P].unsqueeze(1).broadcast_to([P, 8, P]),
                                      headm[:].unsqueeze(2).broadcast_to([P, 8, P]), ALU.mult).then_inc(kM_ready, 1)
                elif name[:2] == "SC":
                    a = int(name[2])
                    dve.wait_ge(post_full, nth(POST, name, g))
                    rows = post[:].rearrange("p (h k) -> p h k", k=NQ)
                    dve.tensor_reduce(smx[:, a, :], rows, AX.X, ALU.max).then_inc(smx_ready, 1)
                    dve.wait_ge(smx_ready, 2 * g + a + 1)
                    dve.tensor_tensor(sc[:, a], rows, smx[:, a, :].unsqueeze(2).broadcast_to([P, SH, NQ]),
                                      ALU.subtract).then_inc(post_free, 1)
                elif name[:2] == "SM":
                    a = int(name[2])
                    dve.wait_ge(sexp_done, 2 * g + a + 1)
                    dve.tensor_reduce(ssm[:, a, :], sc[:, a], AX.X, ALU.add).then_inc(ssum_done, 1)
                    dve.wait_ge(ssum_done, 4 * g + 2 * a + 1)
                    dve.tensor_scalar(ssm[:, a, :], ssm[:, a, :], 1e-12, None, ALU.max).then_inc(ssum_done, 1)
                    dve.wait_ge(ssum_done, 4 * g + 2 * a + 2)
                    dve.reciprocal(rs2[:, a, :], ssm[:, a, :]).then_inc(srecip_done, 1)
                elif name == "VR":
                    dve.wait_ge(post_full, nth(POST, name, g))
                    for r in range(4):
                        rows = slice(r * NQ, (r + 1) * NQ)
                        last = dve.tensor_copy(vb[rows, :, :, r, :],
                                               post[rows].rearrange("p (b c d) -> p b c d", b=GB, c=4))
                    last.then_inc(post_free, 1)
                elif name == "PJ":
                    dve.wait_ge(post_full, nth(POST, name, g))
                    dve.wait_ge(x1b_ready, g + 1)
                    dve.tensor_tensor(x2[:].rearrange("p a c -> p (a c)"), post[:], xb[:].rearrange("p a c -> p (a c)"),
                                      ALU.add).then_inc(post_free, 1)
                elif name[0] == "C":
                    if name == "C0":
                        dve.wait_ge(post_free, nth(POST, "PJ", g))
                    layer_norm(2, int(name[1]), g, x2, hn, 1.0, EPS)
                elif name == "M0":
                    dve.wait_ge(post_free, nth(POST, "T3", g))
                    for s, (mu, mu1) in enumerate(((MUR, MUR1), (MUK, MUK1))):
                        for k in range(2):
                            last = dve.tensor_scalar(mixt[:, 2 * s + k, :].rearrange("p (b q) -> p b q", q=NQ),
                                                     x3T[:, k, :, 0:NQ], cols[:, mu1, k:k + 1], None, ALU.mult)
                    last.then_inc(half_mixed, 1)
                elif name == "M1":
                    dve.wait_ge(half_mixed, g + 1)
                    for s, (mu, mu1) in enumerate(((MUR, MUR1), (MUK, MUK1))):
                        for k in range(2):
                            last = dve.scalar_tensor_tensor(out=mix[:, 2 * s + k, :].rearrange("p (b q) -> p b q", q=NQ),
                                                            in0=x3T[:, k, :, 1:NQ + 1], scalar=cols[:, mu, k:k + 1],
                                                            in1=mixt[:, 2 * s + k, :].rearrange("p (b q) -> p b q", q=NQ),
                                                            op0=ALU.mult, op1=ALU.add)
                    last.then_inc(mixed, 1)
                elif name == "FR":
                    dve.wait_ge(post_full, nth(POST, name, g))
                    after(dve, y_ready, g)
                    dve.tensor_scalar(er.rearrange("p a c -> p (a c)"), post[:], EXP_MAX, None, ALU.max).then_inc(post_free, 1)
                elif name == "SG":
                    dve.wait_ge(er_exp, g + 1)
                    dve.tensor_scalar(er, er, 1.0, None, ALU.add).then_inc(er_one, 1)
                    dve.wait_ge(er_one, g + 1)
                    dve.reciprocal(er, er).then_inc(r_ready, 1)
                elif name == "FV":
                    dve.wait_ge(post_full, nth(POST, name, g))
                    dve.wait_ge(r_ready, g + 1)
                    dve.tensor_tensor(er.rearrange("p a c -> p (a c)"), post[:], er.rearrange("p a c -> p (a c)"),
                                      ALU.mult).then_inc(post_free, 1)

            def group(g, has_pre, has_post):
                for j, name, own in group_jobs(g, has_pre, has_post):
                    if name == "CT":
                        ctx_lower(next_sequence(g, j), *next_context(g, j))
                    elif name in ("S0", "S1", "S2", "S3"):
                        mask_scores(g, j, int(name[1]))
                    elif name in ("R0", "R1"):
                        half = int(name[1])
                        reciprocals(g, j - half, half)
                    elif name in ("P0", "P1"):
                        if name in ON_DVE:
                            prob_copy(g, j - 1, int(name[1]))
                    elif name == "AC":
                        weighed(g, j - 1)
                    elif name in ("LV0", "LV1", "LT"):
                        aux_job(name, g)
                    elif name in FOR_PRE:
                        if name[0] == "A":
                            norm_input(int(name[1]), own)
                        elif name[0] == "K":
                            qk_lower(int(name[1:]), own)
                    elif name not in CORE:
                        post_job(name, own)

            dve.wait_ge(small_in, 16 * N_SMALL)
            dve.tensor_scalar(cols[:, MUR1:MUK1 + 1, :], cols[:, MUR:MUK + 1, :], -1.0, 1.0, ALU.mult, ALU.add).then_inc(consts_made, 1)
            dve.wait_ge(consts_made, 7)
            for stage in range(5):
                norm_input(stage, 0)
            for n in range(len(QK)):
                qk_lower(n, 0)
            ctx_lower(0, "CT0", 0)
            groups(dve, group)
            for name in closing_jobs():
                post_job(name, NG - 1)


_INS = ["x", "ctx_768", "mask_1x1xSxS2_bk0", "L0_xattn_ln_gamma", "L0_xattn_ln_beta", "L0_xattn_Wq", "L0_xattn_Wkv",
        "L0_xattn_Wo", "L0_xattn_bo", "L0_attn_ln_gamma", "L0_attn_ln_beta", "L0_attn_W_qkv", "L0_attn_b_qkv",
        "L0_attn_W_proj", "L0_attn_b_proj", "L0_ffn_W_r", "L0_ffn_W_k", "L0_ffn_W_v", "L0_ffn_mu_r", "L0_ffn_mu_k"]
_OUTS = [((NB, NQ, DM), "float32")]


def kernel(**inputs):
    import numpy as _np
    import concourse.bacc as _bacc
    from concourse import mybir as _mybir
    from concourse.bass_utils import run_bass_kernel_spmd as _run

    nc = _bacc.Bacc("TRN2", target_bir_lowering=False, num_devices=1, dynamic_dma_scratch_size=1024)
    arrays, args = {}, []
    for name in _INS:
        a = _np.ascontiguousarray(inputs[name])
        arrays[f"in_{name}_dram"] = a
        args.append(nc.dram_tensor(f"in_{name}_dram", a.shape, _mybir.dt.from_np(a.dtype), kind="ExternalInput").ap())
    for i, (shape, dtype) in enumerate(_OUTS):
        dt = _mybir.dt.from_np(_np.dtype(dtype))
        args.append(nc.dram_tensor(f"out_{i}_dram", shape, dt, kind="ExternalOutput").ap())
    perceiver_layer(nc, *args)
    r = _run(nc, [arrays], core_ids=[0])
    return r.results[0]["out_0_dram"]
```

```python
from contextlib import ExitStack

import concourse.bass as bass
from concourse import mybir

ALU = mybir.AluOpType
ACT = mybir.ActivationFunctionType
AX = mybir.AxisListType
F32 = mybir.dt.float32
F32R = mybir.dt.float32r
I32 = mybir.dt.int32
U8 = mybir.dt.uint8

P = 128
NB, NQ, DM = 64, 32, 256
NK, DC = 257, 192
NKF = 256
NH, DH = 16, 64
SH, SD = 16, 16
GB = 8
NG = NB // GB
TOK = GB * NQ
XT_TILES = TOK // P
HT = 4
NT = NH // HT
NPAIR = NH // 2
NCTX = 4
EPS = 1e-5
BIG = 3.0e38
MASKED = 1.0e30
EXP_MAX = -87.0
RSQRT_SEED = float(0x5F3759DF)
NEWTON = 3

QK = [job for p in range(0, NPAIR, 2) for job in (("main", p), ("main", p + 1), ("tail", p))]
STEPS = [
    "CU XB OT0 CT S0 R1 N1 P0 OT1 CL A0 S1 U0 A1 OT2 L0 P1 U1 L1 LV0 S2 S3 A2 AC R0 N0 A3 LV1".split(),
    "R1 OT3 CT S0 WO0 N1 P0 CU U0 A4 L0 S1 WO1 CL P1 R0 U1 B0 S2 L1 N0 S3 B1 B2 B3 AC B4".split(),
    "R1 N1 CU X1 S0 P0 T2 S1 XT U0 S2 P1 QT U1 L0 S3 CT L1 Q0 R0 KT AC CL N0 KM0".split(),
    "S0 R1 N1 KM1 VR CT P0 U0 S1 SC0 P1 S2 U1 KM2 R0 L0 E0 KM3 S3 Q1 SM0 CU CL L1 N0 AC".split(),
    "W0 SC1 CU E1 R1 N1 P0 S0 SM1 Q2 PT0 S1 U0 P1 CL S2 W1 R0 PT1 L0 N0 U1 Q3 S3 CT PV L1 AC".split(),
    "R1 N1 P0 CU U0 T4 S0 S1 L0 CT R0 PJ P1 U1 L1 N0 C0 S2 C1 CL C2 S3 C3 AC".split(),
    "C4 CT T3 R1 M0 S0 M1 S1 N1 P0 U0 CU R0 N0 LX L0 S2 FR EZ S3 P1 SG U1 CL FK L1 AC KA".split(),
    "CU R1 N1 P0 S0 U0 L0 S1 R0 P1 CL U1 S2 S3 N0 L1 FV AC".split(),
    "K0 YO K1 R1 N1 K2 P0 K3 U0 K4 L0 P1 LT U1 K5 K6 L1 AC K7 K8 K9 CT K10 K11".split(),
]
CLOSING = (
    "XB OT0 OT1 OT2 OT3 WO0 WO1 B0 B1 B2 B3 B4 T2 X1 KT KM0 QT KM1 SC0 KM2 "
    "KM3 VR E0 SC1 E1 SM0 W0 SM1 W1 PT0 PT1 PV T4 PJ C0 C1 C2 C3 C4 T3 "
    "M0 M1 FR EZ SG FK KA FV YO").split()
FLOW = [name for step in STEPS for name in step]
AUX = ["CT0"]
for j, step in enumerate(STEPS[:GB]):
    AUX += [f"CT{j + 1}" if name == "CT" else name for name in step if name == "CT"]
AUX.append("LT")
PRE = [name for name in FLOW if name in ("XT", "Q0", "Q1", "Q2", "Q3")]
POST = [name for name in FLOW if name in (
    "OT0", "OT1", "OT2", "OT3", "WO0", "WO1", "T2", "QT", "KT", "VR", "SC0", "SC1", "PT0", "PT1", "PV", "T4",
    "PJ", "T3", "FR", "FK", "FV")]
SETUP = "WK0 Q0 WK1 F0 Q1 WK2 F1 Q2 WK3 F2 Q3".split()
SETUP_TRANSPOSES = [name for name in SETUP if name[0] != "Q"]
FOR_PRE = PRE + ["A0", "A1", "A2", "A3", "A4"] + [f"K{n}" for n in range(len(QK))]
CORE = ("CU", "CL", "U0", "U1", "L0", "L1", "CT", "S0", "S1", "S2", "S3", "R0", "R1", "N0", "N1", "P0", "P1", "AC", "LV0", "LV1", "LX", "LT")
ON_DVE = ()
CLOSING_NEEDS = {"WO0": ("OT0", "OT1", "OT2", "OT3"), "QT": ("T2",), "KT": ("T2",), "VR": ("T2",), "SC0": ("QT",), "PV": ("PT0", "PT1", "VR"), "T4": ("PV",),
                 "PJ": ("T4",)}
DVE_POST = ("WO0", "WO1", "VR", "SC0", "SC1", "PJ", "FR", "FV")
LOWER_ON_DVE = ("CL",)
LN_LINKS = 5 + 3 * NEWTON


def perceiver_layer(nc, x, ctx_in, mask, g1, be1, Wq, Wkv, Wo, bo, g2, be2, Wqkv, bqkv, Wproj, bproj,
                    Wr, Wk, Wv, mur, muk, out):
    with ExitStack() as es:
        def sb(name, shape, dt=F32):
            return es.enter_context(nc.sbuf_tensor(name, shape, dt))

        def sem(name):
            return es.enter_context(nc.semaphore(name))

        def psum(name):
            return es.enter_context(nc.psum_tensor(name, [P, 512], F32))

        wq = sb("wq", [P, 2, NH * DH])
        nwk = sb("nwk", [P, NH, P])
        nwkt = sb("nwkt", [P, NPAIR, P])
        wvn = sb("wvn", [P, NH * DH])
        wvb = sb("wvb", [P, NPAIR, P])
        wo = sb("wo", [P, NPAIR, DM])
        wqkv = sb("wqkv", [P, 2, 3 * DM])
        wproj = sb("wproj", [P, 2, DM])
        wrT = sb("wrT", [P, 2, DM])
        wkT = sb("wkT", [P, 2, DM])
        wvT = sb("wvT", [P, 2, DM])
        cols = sb("cols", [P, 8, 2])
        G1, B1, G2, B2, MUR, MUK, MUR1, MUK1 = range(8)
        bcol = sb("bcol", [P, 6])
        bo_row = sb("bo_row", [P, DM])
        bp_row = sb("bp_row", [P, DM])
        ident = sb("ident", [P, P])
        mbias = sb("mbias", [P, NK])
        poison = sb("poison", [P, 2])
        headm = sb("headm", [P, 8])
        seqm = sb("seqm", [NQ, GB])
        leftm = sb("leftm", [P, 4, 4])
        left_h = sb("left_h", [P, 2, NB], F32R)
        left_l = sb("left_l", [P, 2, NB], F32R)
        cx_in = [sb(f"cx_in{r}", [P, 2, 256]) for r in range(NCTX)]
        cT_h = [sb(f"cT_h{r}", [P, 2, NK + 1], F32R) for r in range(2)]
        cT_l = [sb(f"cT_l{r}", [P, 2, NK + 1], F32R) for r in range(2)]
        qk_h = sb("qk_h", [P, GB, NH * NQ], F32R)
        qk_l = sb("qk_l", [P, GB, NH * NQ], F32R)
        qk_t = sb("qk_t", [P, GB, NH * NQ], F32R)
        sm = sb("sm", [P, 2, NK])
        nmx = sb("nmx", [P, 2, NT])
        ssum = sb("ssum", [P, 2, NT])
        rsum = sb("rsum", [P, 2, NT])
        pr = [sb(f"pr{r}", [P, NT, NK]) for r in range(2)]
        prT = sb("prT", [P, 2, NH * NQ])
        prT_h = sb("prT_h", [P, 2, NH * NQ], F32R)
        prT_l = sb("prT_l", [P, 2, NH * NQ], F32R)
        c_h = [sb(f"c_h{r}", [P, 2, P], F32R) for r in range(2)]
        c_l = [sb(f"c_l{r}", [P, 2, P], F32R) for r in range(2)]
        lastp = sb("lastp", [P, NT, GB])
        spread = sb("spread", [P, GB, NQ])
        lvc = sb("lvc", [P, NG, DH])
        lv = sb("lv", [P, NH, DH])
        acm = sb("acm", [P, NH, TOK])
        act_ = sb("act_", [P, NPAIR, TOK])
        xn = sb("xn", [P, 2, DM])
        xnT = sb("xnT", [P, 2, TOK])
        qT = sb("qT", [P, NPAIR, TOK])
        xb = sb("xb", [P, 2, DM])
        x1 = sb("x1", [P, 2, DM])
        x2 = x1
        hn = sb("hn", [P, 2, DM])
        hT = sb("hT", [P, 2, TOK])
        q2T = sb("q2T", [P, 2, TOK])
        kT2 = hn
        kM = sb("kM", [P, 2, 8, P])
        sc = sb("sc", [P, 2, SH, NQ])
        smx = sb("smx", [P, 2, SH])
        ssm = sb("ssm", [P, 2, SH])
        rs2 = sb("rs2", [P, 2, SH])
        vb = sb("vb", [P, GB, 4, 4, SD])
        cv, cvT = hT, q2T
        x3T = sb("x3T", [P, 2, GB, NQ + 1])
        er = sc[:, 0].rearrange("p h k -> p (h k)").rearrange("p (a c) -> p a c", a=2)
        yo = sb("yo", [P, 2, DM])
        st = sb("st", [P, 3, 2, 6])
        mv = sb("mv", [P, 3, 2, 2])
        lw = sb("lw", [P, 3, 4, 2])
        li = sb("li", [P, 3, 2], I32)

        stage = acm[:].rearrange("p h t -> p (h t)")
        wk_main, wk_tail = stage[:, 0:1024], stage[0:64, 1024:2048]
        last_values = kM[0:NB].rearrange("p a b c -> p (a b c)")[:, 0:NH * DH]
        left = kM[:].rearrange("p a b c -> p (a b c)")[:, 1024:1024 + 2 * NB].rearrange("p (k b) -> p k b", k=2)
        mraw = kM[:].rearrange("p a b c -> p (a b c)")[:, 1536:1536 + 128].bitcast(U8)[:, 0:NK]
        spare = kM[:].rearrange("p a b c -> p (a b c)")
        p2T = spare[:, 0:1024].rearrange("p (a c q) -> p a c q", a=2, c=4)
        mixt = spare[:, 0:1024].rearrange("p (s t) -> p s t", s=4)
        mix = spare[:, 1024:2048].rearrange("p (s t) -> p s t", s=4)
        kr = spare[:, 0:512].rearrange("p (k t) -> p k t", k=2)
        ka = spare[:, 512:1024].rearrange("p (k t) -> p k t", k=2)
        ffn_in = [stage[:, 2048 + 512 * n:2560 + 512 * n].rearrange("p (k c) -> p k c", k=2) for n in range(3)]
        left_in = stage[0:NB, 3584:3584 + 256]

        score = [psum("score0"), psum("score1")]
        probT, ac_main, ac_tail, aux, pre, post = (psum(n) for n in ("probT", "ac_main", "ac_tail", "aux", "pre", "post"))
        qk_bank = [score[0], score[1], pre]
        CLOSING_BANKS = [post, pre, aux, ac_main, ac_tail, probT, score[0], score[1]]
        wk_bank, ffn_bank = [ac_main, ac_tail, aux, post], [probT, score[0], score[1]]

        consts_made, ident_made, zeroed = sem("consts_made"), sem("ident_made"), sem("zeroed")
        weights_in, wq_in, mask_in, small_in = sem("weights_in"), sem("wq_in"), sem("mask_in"), sem("small_in")
        wk_staged, ffn_staged = sem("wk_staged"), sem("ffn_staged")
        setup_full, setup_copied, left_upper = sem("setup_full"), sem("setup_copied"), sem("left_upper")
        waits_passed = sem("waits_passed")
        x_in, xres_in, stored = sem("x_in"), sem("xres_in"), sem("stored")
        ctx_loaded = [sem(f"ctx_loaded{r}") for r in range(NCTX)]
        lv_ready, col_ready = sem("lv_ready"), sem("col_ready")
        values_full, values_copied, lvc_in = sem("values_full"), sem("values_copied"), sem("lvc_in")
        aux_full, aux_free = sem("aux_full"), sem("aux_free")
        pre_full, pre_free = sem("pre_full"), sem("pre_free")
        post_full = sem("post_full")
        post_copied = {"ScalarE": sem("post_copied_act"), "VectorE": sem("post_copied_dve")}
        qk_full, qk_upper, qk_split, ctx_upper, kM_ready = (sem(n) for n in ("qk_full", "qk_upper", "qk_split", "ctx_upper", "kM_ready"))
        scores_done, scores_masked, exp_done = sem("scores_done"), sem("scores_masked"), sem("exp_done")
        recip_done, probs_ready, lastp_ready = sem("recip_done"), sem("probs_ready"), sem("lastp_ready")
        probT_full, probT_copied = sem("probT_full"), sem("probT_copied")
        prob_upper, prob_lower = sem("prob_upper"), sem("prob_lower")
        c_upper, c_lower = sem("c_upper"), sem("c_lower")
        ac_done, acm_copied, act_copied = sem("ac_done"), sem("acm_copied"), sem("act_copied")
        ln_link = [sem(f"ln_link{n}") for n in range(3)]
        ln_ready = [sem(f"ln_ready{n}") for n in range(3)]
        xb_ready, x1b_ready, smx_ready = sem("xb_ready"), sem("x1b_ready"), sem("smx_ready")
        sexp_done, ssum_done, srecip_done, p2_ready = sem("sexp_done"), sem("ssum_done"), sem("srecip_done"), sem("p2_ready")
        half_mixed, mixed = sem("half_mixed"), sem("mixed")
        ka_ready, er_exp, er_one, r_ready = sem("ka_ready"), sem("er_exp"), sem("er_one"), sem("r_ready")
        y_ready = sem("y_ready")

        x_rows = x.rearrange("b n c -> (b n) c")
        out_rows = out.rearrange("b n c -> (b n) c")

        def token_rows(t, g):
            return t[bass.ds(g * TOK, TOK), :].rearrange("(a p) c -> p a c", p=P)

        def after(eng, s, value):
            if isinstance(value, int) and value <= 0:
                return
            eng.wait_ge(s, value)

        def alone(eng):
            eng.sem_inc(waits_passed)

        def nth(jobs, name, g):
            return g * len(jobs) + in_order(jobs, g).index(name) + 1

        def in_order(jobs, g):
            if isinstance(g, int) and g == NG - 1 and jobs[0] in CLOSING:
                return sorted(jobs, key=CLOSING.index)
            return jobs

        def groups(eng, group):
            group(0, True, False)
            group(1, True, True)
            with eng.Fori(2, NG - 1) as g:
                group(g, True, True)
            group(NG - 1, False, True)

        def copied(name, g):
            engine = "VectorE" if name in ON_DVE or name in DVE_POST else "ScalarE"
            mine = [n for n in POST if (n in ON_DVE or n in DVE_POST) == (engine == "VectorE")]
            return post_copied[engine], nth(mine, name, g)

        def post_bank(name, g):
            if isinstance(g, int) and g == NG - 1:
                return CLOSING_BANKS[in_order(POST, g).index(name) % len(CLOSING_BANKS)]
            return post

        def group_jobs(g, has_pre, has_post):
            for j, step in enumerate(STEPS):
                for name in step:
                    if name in ("LV0", "LV1") and not (isinstance(g, int) and g == 0):
                        continue
                    if name in CORE:
                        if not (j == 0 and name in ("R1", "N1", "P0", "P1", "U0", "U1", "L0", "L1", "AC")) and not (j == GB and name == "CT" and not has_pre):
                            yield j, name, g
                    elif name in FOR_PRE:
                        if has_pre:
                            yield j, name, g + 1
                    elif has_post:
                        yield j, name, g - 1

        def next_sequence(g, j):
            return g * GB + j + 1 if j < GB else (g + 1) * GB

        def next_context(g, j):
            return (f"CT{j + 1}", g) if j < GB - 1 else ("CT0", g + 1)

        def context_lower(eng, g, j):
            eng.wait_ge(c_upper, g * GB + j + 1)
            eng.tensor_tensor(c_l[j % 2][:], cx_in[j % NCTX][:, :, 0:P], c_h[j % 2][:], ALU.subtract).then_inc(c_lower, 1)

        def prob_lower_part(eng, g, j, half):
            n = 2 * (g * GB + j) + half + 1
            eng.wait_ge(prob_upper, n)
            cut = slice(half * 256, (half + 1) * 256)
            eng.tensor_tensor(prT_l[:, :, cut], prT[:, :, cut], prT_h[:, :, cut], ALU.subtract).then_inc(prob_lower, 1)

        def lower_parts(eng, name, g, j, mine):
            if not mine:
                return
            if name == "CL":
                context_lower(eng, g, j)
            else:
                prob_lower_part(eng, g, j - 1, int(name[1]))

        es.enter_context(nc.allow_non_contiguous_dma(reason="per-channel vectors, one element to a partition"))
        block = es.enter_context(nc.Block())

        N_WEIGHTS, N_STAGED_FFN, N_SMALL, N_SETUP, N_ZEROED = 8, 3, 7, 8, 5

        @block.sync
        def _(sp):
            def load_ctx(b, slot):
                rows = ctx_in[bass.ds(b, 1), 0:NKF, :].rearrange("o (k p) c -> p (o k) c", p=P)
                sp.dma_start(cx_in[slot][:, :, 0:DC], rows).then_inc(ctx_loaded[slot], 16)
                sp.dma_start(cx_in[slot][:, :, DC:256], rows[:, :, P:DC]).then_inc(ctx_loaded[slot], 16)

            def column(v):
                return v.rearrange("(k p) -> p k", p=P)

            sp.dma_start(xn[:], token_rows(x_rows, 0)).then_inc(x_in, 16)
            sp.dma_start(wq[:], Wq.rearrange("(k p) n -> p k n", p=P)).then_inc(wq_in, 16)
            sp.dma_start(wk_main, Wkv[0:P, 0:NH * DH]).then_inc(wk_staged, 16)
            sp.dma_start(wk_tail, Wkv[P:DC, 0:NH * DH]).then_inc(wk_staged, 16)
            sp.dma_start(left_in[:, 0:DC], ctx_in[:, NKF, :]).then_inc(wk_staged, 16)
            sp.dma_start(left_in[:, DC:256], ctx_in[:, NKF, P:DC]).then_inc(wk_staged, 16)
            for n, v in ((G1, g1), (B1, be1), (G2, g2), (B2, be2), (MUR, mur), (MUK, muk)):
                sp.dma_start(cols[:, n, :], column(v)).then_inc(small_in, 16)
            sp.dma_start(bcol[:], column(bqkv)).then_inc(small_in, 16)
            for n, w in enumerate((Wr, Wk, Wv)):
                sp.dma_start(ffn_in[n], w.rearrange("(k p) c -> p k c", p=P)).then_inc(ffn_staged, 16)
            for r in range(4):
                sp.dma_start(mraw[r * NQ:(r + 1) * NQ, :], mask[0, 0, :, :]).then_inc(mask_in, 16)
            for r in range(NCTX):
                load_ctx(r, r)
            sp.wait_ge(zeroed, 2)
            wv_all = Wkv[:, NH * DH:2 * NH * DH]
            sp.dma_start(wvn[:], wv_all[0:P, :]).then_inc(weights_in, 16)
            tails = wv_all[P:DC, :].rearrange("c (n r d) -> c n r d", r=2, d=DH)
            for r in range(2):
                sp.dma_start(wvb[r * 64:r * 64 + 64, :, r * 64:r * 64 + 64], tails[:, :, r, :]).then_inc(weights_in, 16)
            sp.dma_start(wo[:], Wo.rearrange("(k p) n -> p k n", p=P)).then_inc(weights_in, 16)
            sp.dma_start(wqkv[:], Wqkv.rearrange("(k p) n -> p k n", p=P)).then_inc(weights_in, 16)
            sp.dma_start(wproj[:], Wproj.rearrange("(k p) n -> p k n", p=P)).then_inc(weights_in, 16)
            sp.dma_start(bo_row[:], bo.partition_broadcast(P)).then_inc(weights_in, 16)
            sp.dma_start(bp_row[:], bproj.partition_broadcast(P)).then_inc(weights_in, 16)

            def store(g):
                sp.wait_ge(y_ready, g + 1)
                sp.dma_start(token_rows(out_rows, g), yo[:]).then_inc(stored, 16)

            def load_residual(g):
                after(sp, y_ready, g)
                sp.dma_start(xb[:], token_rows(x_rows, g)).then_inc(xres_in, 16)

            def spread_last_values():
                sp.wait_ge(values_copied, 2)
                for h in range(NH):
                    row = ((h % 4) * 4 + h // 4) * GB
                    sp.dma_start(lvc[row:row + GB], last_values[:, h * DH:(h + 1) * DH]).then_inc(lvc_in, 16)

            def group(g, has_pre, has_post):
                if has_pre:
                    sp.wait_ge(pre_full, nth(PRE, "XT", g))
                    sp.dma_start(xn[:], token_rows(x_rows, g + 1)).then_inc(x_in, 16)
                if has_post:
                    load_residual(g - 1)
                else:
                    spread_last_values()
                for j in range(GB if has_pre else GB - NCTX):
                    sp.wait_ge(ac_done, g * GB + j + 1)
                    load_ctx(g * GB + j + NCTX, j % NCTX)
                if has_post:
                    store(g - 1)

            groups(sp, group)
            load_residual(NG - 1)
            store(NG - 1)
            sp.wait_ge(stored, 16 * NG)

        @block.gpsimd
        def _(pool):
            pool.memset(ident[:], 0.0).then_inc(ident_made, 1)
            pool.wait_ge(ident_made, 1)
            pool.affine_select(out=ident[:], in_=ident[:], compare_op=ALU.not_equal, fill=1.0, base=0,
                               pattern=[[-1, P]], channel_multiplier=1).then_inc(ident_made, 1)
            pool.memset(nwk[:], 0.0)
            pool.memset(nwkt[:], 0.0).then_inc(zeroed, 1)
            pool.memset(wvb[:], 0.0).then_inc(zeroed, 1)
            for r in range(2):
                pool.memset(cT_h[r][:, :, NK].bitcast(F32), 0.0)
                last = pool.memset(cT_l[r][:, :, NK].bitcast(F32), 0.0)
            last.then_inc(zeroed, 1)
            pool.memset(vb[:], 0.0).then_inc(zeroed, 1)
            pool.memset(x3T[:, :, :, 0], 0.0).then_inc(zeroed, 1)

            def columns(b, name):
                after(pool, scores_done, (b - 1) * NT)
                alone(pool)
                r = int(name[2]) % 2
                pool.tensor_copy(cT_h[r][:, :, NKF], left_h[:, :, bass.ds(b, 1)].rearrange("p k o -> p (k o)"))
                pool.tensor_copy(cT_l[r][:, :, NKF], left_l[:, :, bass.ds(b, 1)].rearrange("p k o -> p (k o)")).then_inc(col_ready, 1)

            def spread_values(g):
                if isinstance(g, int) and g == 0:
                    pool.wait_ge(lvc_in, 16 * NH)
                after(pool, post_full, nth(POST, "OT3", g - 1))
                alone(pool)
                keep = leftm[:].rearrange("p t r -> p (t r)").unsqueeze(2).broadcast_to([P, NH, DH])
                mine = lvc[:, bass.ds(g, 1), :].broadcast_to([P, NH, DH])
                pool.tensor_tensor(lv[:], mine, keep, ALU.mult).then_inc(lv_ready, 1)

            def normalise(g, j, half):
                pool.wait_ge(recip_done, 2 * (g * GB + j) + half + 1)
                alone(pool)
                for t in (2 * half, 2 * half + 1):
                    p = pr[j % 2][:, t, :]
                    last = pool.tensor_scalar(p, p, rsum[:, j % 2, t:t + 1], poison[:, 0:1], ALU.mult, ALU.mult)
                last.then_inc(probs_ready, 1)
                if half == 1:
                    if j == 0:
                        after(pool, aux_full, g * len(AUX))
                    pool.wait_ge(probs_ready, 2 * (g * GB + j) + 2)
                    alone(pool)
                    pool.tensor_copy(lastp[:, :, j], pr[j % 2][:, :, NKF]).then_inc(lastp_ready, 1)

            def job(name, g):
                if name == "XB":
                    pool.wait_ge(xres_in, 16 * (g + 1))
                    for a in range(2):
                        last = pool.tensor_tensor(xb[:, a, :], xb[:, a, :], bo_row[:], ALU.add)
                    last.then_inc(xb_ready, 1)
                elif name == "X1":
                    pool.wait_ge(*copied("WO1", g))
                    for a in range(2):
                        last = pool.tensor_tensor(xb[:, a, :], x1[:, a, :], bp_row[:], ALU.add)
                    last.then_inc(x1b_ready, 1)
                elif name in ("W0", "W1"):
                    a = int(name[1])
                    pool.wait_ge(srecip_done, 2 * g + a + 1)
                    pool.tensor_tensor(sc[:, a], sc[:, a], rs2[:, a, :].unsqueeze(2).broadcast_to([P, SH, NQ]),
                                       ALU.mult).then_inc(p2_ready, 1)
                elif name == "KA":
                    pool.wait_ge(*copied("FK", g))
                    pool.tensor_tensor(ka, kr, kr, ALU.mult).then_inc(ka_ready, 1)
                elif name == "YO":
                    pool.wait_ge(*copied("FV", g))
                    after(pool, stored, 16 * g)
                    pool.tensor_tensor(yo[:], er, x2[:], ALU.add).then_inc(y_ready, 1)

            def group(g, has_pre, has_post):
                for j, name, own in group_jobs(g, has_pre, has_post):
                    if name == "CT":
                        columns(next_sequence(g, j), next_context(g, j)[0])
                    elif name in ("N0", "N1"):
                        half = int(name[1])
                        normalise(g, j - half, half)
                    elif name == "LX":
                        spread_values(g)
                    elif name in ("CL", "L0", "L1"):
                        lower_parts(pool, name, g, j, name not in LOWER_ON_DVE)
                    else:
                        job(name, own)

            pool.wait_ge(setup_copied, N_SETUP)
            pool.wait_ge(consts_made, 8)
            pool.wait_ge(weights_in, 16 * N_WEIGHTS)
            columns(0, "CT0")
            groups(pool, group)
            for name in CLOSING:
                job(name, NG - 1)

        @block.tensor
        def _(pe):
            def transposes(bank, src):
                for a in range(2):
                    for k in range(2):
                        last = pe.transpose(bank[:, k * TOK + a * P:k * TOK + (a + 1) * P], src[:, a, k * P:(k + 1) * P], ident[:])
                return last

            def pre_job(name, g):
                after(pe, pre_free, nth(PRE, name, g) - 1)
                if name == "XT":
                    after(pe, qk_split, g * len(QK))
                if name == "XT":
                    pe.wait_ge(ln_ready[0], g + 1)
                    last = transposes(pre, xn)
                else:
                    n = int(name[1])
                    for i in range(2):
                        for k in range(2):
                            last = pe.matmul(pre[:, i * TOK:(i + 1) * TOK], wq[:, k, (2 * n + i) * P:(2 * n + i + 1) * P],
                                             xnT[:, k, :], start=(k == 0), stop=(k == 1))
                last.then_inc(pre_full, 1)

            def qk_job(n, g):
                bank = qk_bank[n % 3]
                if n == 0:
                    after(pe, scores_masked, g * GB * NT)
                    pe.wait_ge(pre_free, nth(PRE, "Q3", g))
                if n >= 3:
                    pe.wait_ge(qk_split, g * len(QK) + n - 2)
                kind, p = QK[n]
                for i in range(2):
                    half = bank[:, i * TOK:(i + 1) * TOK]
                    if kind == "main":
                        last = pe.matmul(half, nwk[:, 2 * p + i, :], qT[:, p, :], start=True, stop=True)
                    else:
                        last = pe.matmul(half, nwkt[:, p + i, :], qT[:, p + i, :], start=True, stop=True)
                last.then_inc(qk_full, 1)

            def aux_job(name, g):
                after(pe, aux_free, nth(AUX, name, g) - 1)
                if name[:2] == "CT":
                    j = int(name[2])
                    pe.wait_ge(ctx_loaded[j % NCTX], g * 32 * (GB // NCTX) + 32 * (j // NCTX + 1))
                    for m in range(2):
                        for k in range(2):
                            last = pe.transpose(aux[:, k * NKF + m * P:k * NKF + (m + 1) * P],
                                                cx_in[j % NCTX][:, m, k * P:(k + 1) * P], ident[:])
                else:
                    pe.wait_ge(lastp_ready, (g + 1) * GB)
                    last = pe.transpose(aux[0:NT * GB, 0:P], lastp[:].rearrange("p t b -> p (t b)"), ident[:])
                last.then_inc(aux_full, 1)

            def last_row_values(n):
                if n == 1:
                    pe.wait_ge(values_copied, 1)
                for k, w in enumerate((wvn[:], wvb[:].rearrange("p n c -> p (n c)"))):
                    last = pe.matmul(post[0:NB, :], left[:, k, :], w[:, n * 512:(n + 1) * 512], start=(k == 0), stop=(k == 1))
                last.then_inc(values_full, 1)

            def scores(g, j, t):
                n = j * NT + t
                if n == 0:
                    pe.wait_ge(qk_split, (g + 1) * len(QK))
                elif n >= 2:
                    pe.wait_ge(scores_masked, g * GB * NT + n - 1)
                if t == 0:
                    pe.wait_ge(aux_free, nth(AUX, f"CT{j}", g))
                    pe.wait_ge(col_ready, g * GB + j + 1)
                tile = slice(t * P, (t + 1) * P)
                c_h, c_l = cT_h[j % 2], cT_l[j % 2]
                products = [(qk_h, c_h[:, 0]), (qk_h, c_l[:, 0]), (qk_l, c_h[:, 0]), (qk_t, c_h[:, 1]), (qk_t, c_l[:, 1])]
                for i, (q, c) in enumerate(products):
                    last = pe.matmul(score[t % 2][:, 0:NK + 1], q[:, j, tile], c, start=(i == 0), stop=(i == len(products) - 1))
                last.then_inc(scores_done, 1)

            def prob_transposes(g, j, half):
                n = 2 * (g * GB + j) + half
                pe.wait_ge(probs_ready, n + 1)
                after(pe, probT_copied, n)
                for m in range(2):
                    for i in range(2):
                        last = pe.transpose(probT[:, m * 256 + i * P:m * 256 + (i + 1) * P],
                                            pr[j % 2][:, 2 * half + i, m * P:(m + 1) * P], ident[:])
                last.then_inc(probT_full, 1)

            def weigh(g, j):
                n = 2 * (g * GB + j) + 2
                after(pe, acm_copied, g * GB + j)
                after(pe, act_copied, g * GB + j)
                pe.wait_ge(probT_copied, n)
                for m in range(2):
                    by_pair = prT[:, m, :].rearrange("p (n r q) -> p n r q", r=2, q=NQ)
                    for r in range(2):
                        pe.matmul(ac_tail[r * 64:r * 64 + 64, 0:TOK], cx_in[j % NCTX][:, m, P:DC], by_pair[:, :, r, :],
                                  start=(m == 0), stop=(m == 1))
                pe.wait_ge(c_lower, g * GB + j + 1)
                pe.wait_ge(prob_upper, n)
                for m in range(2):
                    pe.matmul(ac_main[:], c_h[j % 2][:, m, :], prT_h[:, m, :], start=(m == 0), stop=False)
                    pe.matmul(ac_main[:], c_l[j % 2][:, m, :], prT_h[:, m, :], start=False, stop=False)
                pe.wait_ge(prob_lower, n)
                for m in range(2):
                    last = pe.matmul(ac_main[:], c_h[j % 2][:, m, :], prT_l[:, m, :], start=False, stop=(m == 1))
                last.then_inc(ac_done, 1)

            def post_job(name, g):
                if name not in POST:
                    return
                bank = post_bank(name, g)
                order = in_order(POST, g)
                n = order.index(name)
                if isinstance(g, int) and g == NG - 1:
                    for need in CLOSING_NEEDS.get(name, ()):
                        pe.wait_ge(*copied(need, g))
                    if n == 0:
                        pe.wait_ge(*copied(POST[-1], g - 1))
                    if n >= len(CLOSING_BANKS):
                        pe.wait_ge(*copied(order[n - len(CLOSING_BANKS)], g))
                elif n > 0:
                    pe.wait_ge(*copied(order[n - 1], g))
                else:
                    after(pe, *copied(POST[-1], g - 1))
                if name[:2] == "SC":
                    pe.wait_ge(kM_ready, 4 * g + 2 * int(name[2]) + 2)
                if name[:2] == "OT":
                    n = int(name[2])
                    if n == 0:
                        pe.wait_ge(acm_copied, (g + 1) * GB)
                        pe.wait_ge(act_copied, (g + 1) * GB)
                        pe.wait_ge(aux_free, (g + 1) * len(AUX))
                        pe.wait_ge(lv_ready, g + 1)
                        pe.wait_ge(values_copied, 2)
                    for i in range(2):
                        p, half = 2 * n + i, slice(i * TOK, (i + 1) * TOK)
                        for r in range(2):
                            pe.matmul(bank[r * 64:r * 64 + 64, half], wvn[:, (2 * p + r) * DH:(2 * p + r + 1) * DH],
                                      acm[:, 2 * p + r, :], start=True, stop=False)
                        pe.matmul(bank[:, half], wvb[:, p, :], act_[:, p, :], start=False, stop=False)
                        last = pe.matmul(bank[:, half], lv[:, 2 * p:2 * p + 2, :].rearrange("p h d -> p (h d)"),
                                         spread[:].rearrange("p b q -> p (b q)"), start=False, stop=True)
                elif name[:2] == "WO":
                    a = int(name[2])
                    for k in range(NPAIR):
                        last = pe.matmul(bank[:, 0:DM], qT[:, k, a * P:(a + 1) * P], wo[:, k, :],
                                         start=(k == 0), stop=(k == NPAIR - 1))
                elif name == "T2":
                    pe.wait_ge(ln_ready[1], g + 1)
                    last = transposes(bank, hn)
                elif name in ("QT", "KT"):
                    for c in range(2):
                        w0 = (0 if name == "QT" else DM) + c * P
                        for k in range(2):
                            last = pe.matmul(bank[:, c * TOK:(c + 1) * TOK], wqkv[:, k, w0:w0 + P], hT[:, k, :],
                                             start=(k == 0), stop=(k == 1))
                elif name[:2] == "SC":
                    a = int(name[2])
                    for c in range(2):
                        for b in range(4):
                            at = (a * 4 + b) * NQ
                            last = pe.matmul(bank[b * NQ:(b + 1) * NQ, c * 256:(c + 1) * 256], q2T[:, c, at:at + NQ],
                                             kM[:, c, :, b * NQ:(b + 1) * NQ], start=True, stop=True)
                elif name == "VR":
                    for k in range(2):
                        vw = wqkv[:, k, 2 * DM:3 * DM].rearrange("p (c r d) -> p c r d", c=4, r=4)
                        for b in range(GB):
                            for r in range(4):
                                last = pe.matmul(bank[r * NQ:(r + 1) * NQ, b * 64:(b + 1) * 64], hT[:, k, b * NQ:(b + 1) * NQ],
                                                 vw[:, :, r, :], start=(k == 0 and b == 0), stop=(k == 1), skip_group_check=True)
                elif name[:2] == "PT":
                    a = int(name[2])
                    pe.wait_ge(p2_ready, 2 * g + a + 1)
                    flat = sc[:, a].rearrange("p h k -> p (h k)")
                    for c in range(4):
                        last = pe.transpose(bank[:, c * P:(c + 1) * P], flat[:, c * P:(c + 1) * P], ident[:])
                elif name == "PV":
                    for a in range(2):
                        for c in range(4):
                            for b in range(4):
                                last = pe.matmul(bank[b * NQ:(b + 1) * NQ, a * DM + c * 64:a * DM + (c + 1) * 64],
                                                 p2T[:, a, c, b * NQ:(b + 1) * NQ],
                                                 vb[:, a * 4 + b, c].rearrange("p r d -> p (r d)"), start=True, stop=True)
                elif name == "T4":
                    last = transposes(bank, cv)
                elif name == "PJ":
                    for a in range(2):
                        for k in range(2):
                            last = pe.matmul(bank[:, a * DM:(a + 1) * DM], cvT[:, k, a * P:(a + 1) * P], wproj[:, k, :],
                                             start=(k == 0), stop=(k == 1))
                elif name == "T3":
                    pe.wait_ge(ln_ready[2], g + 1)
                    last = transposes(bank, hn)
                elif name == "FK":
                    pe.wait_ge(mixed, 2 * g + 2)
                    for m in range(2):
                        for k in range(2):
                            last = pe.matmul(bank[:, m * TOK:(m + 1) * TOK], wkT[:, k, m * P:(m + 1) * P], mix[:, 2 + k, :],
                                             start=(k == 0), stop=(k == 1))
                elif name == "FR":
                    pe.wait_ge(mixed, 2 * g + 1)
                    for a in range(2):
                        for k in range(2):
                            last = pe.matmul(bank[:, a * DM:(a + 1) * DM], mix[:, k, a * P:(a + 1) * P], wrT[:, k, :],
                                             start=(k == 0), stop=(k == 1))
                elif name == "FV":
                    pe.wait_ge(ka_ready, g + 1)
                    for a in range(2):
                        for k in range(2):
                            last = pe.matmul(bank[:, a * DM:(a + 1) * DM], ka[:, k, a * P:(a + 1) * P], wvT[:, k, :],
                                             start=(k == 0), stop=(k == 1))
                last.then_inc(post_full, 1)

            def group(g, has_pre, has_post):
                for j, name, own in group_jobs(g, has_pre, has_post):
                    if name == "CT":
                        aux_job(*next_context(g, j))
                    elif name in ("LV0", "LV1"):
                        last_row_values(int(name[2]))
                    elif name == "LT":
                        aux_job(name, g)
                    elif name in ("S0", "S1", "S2", "S3"):
                        scores(g, j, int(name[1]))
                    elif name in ("P0", "P1"):
                        prob_transposes(g, j - 1, int(name[1]))
                    elif name == "AC":
                        weigh(g, j - 1)
                    elif name in PRE:
                        pre_job(name, own)
                    elif name[0] == "K" and name in FOR_PRE:
                        qk_job(int(name[1:]), own)
                    else:
                        post_job(name, own)

            pe.wait_ge(ident_made, 2)
            pre_job("XT", 0)
            pe.wait_ge(wk_staged, 64)
            for name in SETUP:
                n = int(name[-1])
                if name[:2] == "WK":
                    if n == 0:
                        pe.transpose(wk_bank[0][:, 2 * DC:2 * DC + NB], left_in[:, 0:P], ident[0:NB, 0:NB])
                        pe.transpose(wk_bank[0][:, 2 * DC + NB:2 * DC + 2 * NB], left_in[:, P:256], ident[0:NB, 0:NB])
                    for i in range(2):
                        pair = slice((2 * n + i) * P, (2 * n + i + 1) * P)
                        pe.transpose(wk_bank[n][:, i * DC:i * DC + P], wk_main[:, pair], ident[:])
                        last = pe.transpose(wk_bank[n][:, i * DC + P:(i + 1) * DC], wk_tail[:, pair], ident[0:64, 0:64])
                elif name[0] == "F":
                    if n == 0:
                        pe.wait_ge(ffn_staged, 16 * N_STAGED_FFN)
                    for kd in range(2):
                        for kc in range(2):
                            last = pe.transpose(ffn_bank[n][:, kc * DM + kd * P:kc * DM + (kd + 1) * P],
                                                ffn_in[n][:, kd, kc * P:(kc + 1) * P], ident[:])
                else:
                    if n == 0:
                        pe.wait_ge(wq_in, 16)
                    pre_job(name, 0)
                    continue
                last.then_inc(setup_full, 1)
            pe.wait_ge(setup_copied, N_SETUP)
            for n in range(len(QK)):
                if n == 9:
                    aux_job("CT0", 0)
                qk_job(n, 0)
            pe.wait_ge(zeroed, N_ZEROED)
            pe.wait_ge(weights_in, 16 * N_WEIGHTS)
            pe.wait_ge(small_in, 16 * N_SMALL)
            groups(pe, group)
            for name in CLOSING:
                post_job(name, NG - 1)

        @block.scalar
        def _(act):
            def pre_job(name, g):
                act.wait_ge(pre_full, nth(PRE, name, g))
                if name == "XT":
                    for k in range(2):
                        last = act.activation(xnT[:, k, :], pre[:, k * TOK:(k + 1) * TOK], ACT.Identity,
                                              bias=cols[:, B1, k:k + 1], scale=cols[:, G1, k:k + 1])
                else:
                    n = int(name[1])
                    last = act.activation(qT[:, 2 * n:2 * n + 2, :].rearrange("p n t -> p (n t)"), pre[:], ACT.Copy)
                last.then_inc(pre_free, 1)

            def qk_copy(n, g):
                act.wait_ge(qk_full, g * len(QK) + n + 1)
                kind, p = QK[n]
                src = qk_bank[n % 3][:].rearrange("p (i b q) -> p b i q", i=2, q=NQ)
                if kind == "main":
                    dst = qk_h[:, :, 2 * p * NQ:(2 * p + 2) * NQ].rearrange("p b (i q) -> p b i q", q=NQ)
                    act.activation(dst, src, ACT.Copy).then_inc(qk_upper, 1)
                else:
                    for r in range(2):
                        rows = slice(r * 64, r * 64 + 64)
                        dst = qk_t[rows, :, 2 * p * NQ:(2 * p + 4) * NQ].rearrange("p b (i r q) -> p b i r q", r=2, q=NQ)[:, :, :, r]
                        last = act.activation(dst, src[rows], ACT.Copy)
                    last.then_inc(qk_upper, 1)

            def context(b, name, g):
                act.wait_ge(aux_full, nth(AUX, name, g))
                after(act, scores_done, (b - 1) * NT)
                r = int(name[2]) % 2
                act.activation(cT_h[r][:, :, 0:NKF], aux[:].rearrange("p (k m) -> p k m", k=2), ACT.Copy).then_inc(ctx_upper, 1)

            def exponent(g, j, t):
                act.wait_ge(scores_masked, g * GB * NT + j * NT + t + 1)
                if t == 0:
                    after(act, probT_full, 2 * (g * GB + j - 1))
                    after(act, lastp_ready, g * GB + j - 1)
                act.activation(pr[j % 2][:, t, :], sm[:, t % 2, :], ACT.Exp, bias=nmx[:, j % 2, t:t + 1], scale=-1.0,
                               accum_out=ssum[:, j % 2, t:t + 1]).then_inc(exp_done, 1)

            def prob_copy(g, j, half):
                act.wait_ge(probT_full, 2 * (g * GB + j) + half + 1)
                if half == 0:
                    after(act, ac_done, g * GB + j)
                act.activation(prT[:, :, half * 256:(half + 1) * 256], probT[:].rearrange("p (m c) -> p m c", m=2),
                               ACT.Copy).then_inc(probT_copied, 1)

            def prob_upper_part(g, j, half):
                act.wait_ge(probT_copied, 2 * (g * GB + j) + half + 1)
                cut = slice(half * 256, (half + 1) * 256)
                act.activation(prT_h[:, :, cut], prT[:, :, cut], ACT.Copy).then_inc(prob_upper, 1)

            def context_upper(g, j):
                act.wait_ge(aux_full, nth(AUX, f"CT{j}", g))
                after(act, ac_done, g * GB + j - 1)
                act.activation(c_h[j % 2][:], cx_in[j % NCTX][:, :, 0:P], ACT.Copy).then_inc(c_upper, 1)

            def weighed(g, j):
                act.wait_ge(ac_done, g * GB + j + 1)
                act.activation(acm[:, :, j * NQ:(j + 1) * NQ], ac_main[:].rearrange("p (h q) -> p h q", q=NQ),
                               ACT.Copy).then_inc(acm_copied, 1)

            def post_job(name, g):
                if name in ON_DVE or name not in ("OT0", "OT1", "OT2", "OT3", "T2", "QT", "KT", "E0", "E1", "PT0", "PT1", "PV", "T4", "T3", "M0", "FK", "EZ"):
                    return
                if name in ("E0", "E1"):
                    a = int(name[1])
                    act.wait_ge(*copied(f"SC{a}", g))
                    act.activation(sc[:, a], sc[:, a], ACT.Exp, scale=float(SD) ** -0.5).then_inc(sexp_done, 1)
                    return
                if name == "M0":
                    act.wait_ge(*copied("T3", g))
                    for n, mu1 in enumerate((MUR1, MUK1)):
                        for k in range(2):
                            last = act.activation(mixt[:, 2 * n + k, :].rearrange("p (b q) -> p b q", q=NQ), x3T[:, k, :, 0:NQ],
                                                  ACT.Copy, scale=cols[:, mu1, k:k + 1])
                        last.then_inc(half_mixed, 1)
                    return
                if name == "EZ":
                    act.wait_ge(*copied("FR", g))
                    act.activation(er, er, ACT.Exp, scale=-1.0).then_inc(er_exp, 1)
                    return
                bank = post_bank(name, g)
                act.wait_ge(post_full, nth(POST, name, g))
                if name[:2] == "OT":
                    n = int(name[2])
                    last = act.activation(qT[:, 2 * n:2 * n + 2, :].rearrange("p n t -> p (n t)"), bank[:], ACT.Copy)
                elif name == "T2":
                    for k in range(2):
                        last = act.activation(hT[:, k, :], bank[:, k * TOK:(k + 1) * TOK], ACT.Identity,
                                              bias=cols[:, B2, k:k + 1], scale=cols[:, G2, k:k + 1])
                elif name == "QT":
                    for k in range(2):
                        last = act.activation(q2T[:, k, :], bank[:, k * TOK:(k + 1) * TOK], ACT.Identity, bias=bcol[:, k:k + 1])
                elif name == "KT":
                    for k in range(2):
                        last = act.activation(kT2[:, k, :], bank[:, k * TOK:(k + 1) * TOK], ACT.Identity, bias=bcol[:, 2 + k:3 + k])
                elif name[:2] == "PT":
                    last = act.activation(p2T[:, int(name[2])].rearrange("p c q -> p (c q)"), bank[:], ACT.Copy)
                elif name == "PV":
                    last = act.activation(cv[:].rearrange("p a c -> p (a c)"), bank[:], ACT.Copy)
                elif name == "T4":
                    for k in range(2):
                        last = act.activation(cvT[:, k, :], bank[:, k * TOK:(k + 1) * TOK], ACT.Identity, bias=bcol[:, 4 + k:5 + k])
                elif name == "T3":
                    last = act.activation(x3T[:, :, :, 1:NQ + 1], bank[:].rearrange("p (k b q) -> p k b q", k=2, q=NQ), ACT.Copy)
                elif name == "FK":
                    after(act, ka_ready, g)
                    last = act.activation(kr.rearrange("p k t -> p (k t)"), bank[:], ACT.Relu)
                last.then_inc(post_copied["ScalarE"], 1)

            def group(g, has_pre, has_post):
                for j, name, own in group_jobs(g, has_pre, has_post):
                    if name == "CT":
                        context(next_sequence(g, j), *next_context(g, j))
                    elif name in ("S0", "S1", "S2", "S3"):
                        exponent(g, j, int(name[1]))
                    elif name in ("P0", "P1"):
                        if name not in ON_DVE:
                            prob_copy(g, j - 1, int(name[1]))
                    elif name in ("U0", "U1"):
                        prob_upper_part(g, j - 1, int(name[1]))
                    elif name in ("LV0", "LV1"):
                        n = int(name[2])
                        act.wait_ge(values_full, n + 1)
                        act.activation(last_values[:, n * 512:(n + 1) * 512], post[0:NB, :], ACT.Copy).then_inc(values_copied, 1)
                    elif name == "CU":
                        context_upper(g, j)
                    elif name == "AC":
                        weighed(g, j - 1)
                    elif name in PRE:
                        pre_job(name, own)
                    elif name[0] == "K" and name in FOR_PRE:
                        qk_copy(int(name[1:]), own)
                    elif name not in CORE:
                        post_job(name, own)

            act.wait_ge(small_in, 16 * N_SMALL)
            pre_job("XT", 0)
            act.wait_ge(setup_full, 1)
            last_rows = wk_bank[0][:, 2 * DC:2 * DC + 2 * NB]
            act.activation(left[:].rearrange("p k (b g) -> p k g b", g=NG), last_rows.rearrange("p (k g b) -> p k g b", k=2, g=NG), ACT.Copy)
            act.activation(left_h[:].rearrange("p k b -> p (k b)"), last_rows, ACT.Copy).then_inc(left_upper, 1)
            for n, w in enumerate((wrT, wkT, wvT)):
                pre_job(PRE[1 + n], 0)
                act.wait_ge(setup_full, SETUP_TRANSPOSES.index(f"F{n}") + 1)
                act.activation(w[:].rearrange("p k d -> p (k d)"), ffn_bank[n][:], ACT.Copy).then_inc(setup_copied, 1)
            pre_job(PRE[4], 0)
            for n in range(len(QK)):
                if n == 9:
                    context(0, "CT0", 0)
                qk_copy(n, 0)
            groups(act, group)
            for name in CLOSING:
                post_job(name, NG - 1)

        @block.vector
        def _(dve):
            def layer_norm(n, stage, g, src, dst, scale, shift):
                def linked(i):
                    dve.wait_ge(ln_link[n], g * LN_LINKS + i)

                w, y, q = lw[:, n, 0, :], lw[:, n, 1, :], lw[:, n, 2, :]
                if stage == 0:
                    dve.bn_stats(st[:, n, 0, :], src[:, 0, :])
                    dve.bn_stats(st[:, n, 1, :], src[:, 1, :]).then_inc(ln_link[n], 1)
                    linked(1)
                    alone(dve)
                    dve.bn_aggr(mv[:, n, 0, :], st[:, n, 0, :])
                    dve.bn_aggr(mv[:, n, 1, :], st[:, n, 1, :]).then_inc(ln_link[n], 1)
                elif stage < 4:
                    if stage == 1:
                        linked(2)
                        dve.tensor_scalar(w, mv[:, n, :, 1], scale, shift, ALU.mult, ALU.add).then_inc(ln_link[n], 1)
                        linked(3)
                        dve.tensor_scalar(li[:, n, :], w.bitcast(I32), 1, None, ALU.logical_shift_right).then_inc(ln_link[n], 1)
                        linked(4)
                        dve.tensor_scalar(y.bitcast(I32), li[:, n, :], -1.0, RSQRT_SEED, ALU.mult, ALU.add).then_inc(ln_link[n], 1)
                    i = 5 + 3 * (stage - 1)
                    linked(i)
                    dve.tensor_tensor(q, y, y, ALU.mult).then_inc(ln_link[n], 1)
                    linked(i + 1)
                    dve.scalar_tensor_tensor(out=q, in0=q, scalar=-0.5, in1=w, op0=ALU.mult, op1=ALU.mult).then_inc(ln_link[n], 1)
                    linked(i + 2)
                    dve.scalar_tensor_tensor(out=y, in0=q, scalar=1.5, in1=y, op0=ALU.add, op1=ALU.mult).then_inc(ln_link[n], 1)
                else:
                    linked(LN_LINKS)
                    for a in range(2):
                        last = dve.tensor_scalar(dst[:, a, :], src[:, a, :], mv[:, n, a, 0:1], y[:, a:a + 1],
                                                 ALU.subtract, ALU.mult)
                    last.then_inc(ln_ready[n], 1)

            def norm_input(stage, g):
                if stage == 0:
                    dve.wait_ge(x_in, 16 * (g + 1))
                layer_norm(0, stage, g, xn, xn, 1.0 + EPS, EPS * EPS)

            def qk_lower(n, g):
                dve.wait_ge(qk_upper, g * len(QK) + n + 1)
                kind, p = QK[n]
                src = qk_bank[n % 3][:].rearrange("p (i b q) -> p b i q", i=2, q=NQ)
                if kind == "main":
                    upper, dst = (t[:, :, 2 * p * NQ:(2 * p + 2) * NQ].rearrange("p b (i q) -> p b i q", q=NQ) for t in (qk_h, qk_l))
                    dve.tensor_tensor(dst, src, upper, ALU.subtract).then_inc(qk_split, 1)
                else:
                    heads = qk_t[:, :, 2 * p * NQ:(2 * p + 4) * NQ].rearrange("p b (i r q) -> p b i r q", r=2, q=NQ)
                    for r in range(2):
                        own, other = slice(r * 64, r * 64 + 64), slice(64 - r * 64, 128 - r * 64)
                        last = dve.tensor_tensor(heads[other, :, :, r], src[own], heads[own, :, :, r], ALU.subtract)
                    last.then_inc(qk_split, 1)

            def ctx_lower(b, name, g):
                dve.wait_ge(ctx_upper, b + 1)
                r = int(name[2]) % 2
                dve.tensor_tensor(cT_l[r][:, :, 0:NKF], aux[:].rearrange("p (k m) -> p k m", k=2),
                                  cT_h[r][:, :, 0:NKF], ALU.subtract).then_inc(aux_free, 1)

            def mask_scores(g, j, t):
                n = g * GB * NT + j * NT + t
                dve.wait_ge(scores_done, n + 1)
                after(dve, exp_done, n - 1)
                alone(dve)
                dve.tensor_tensor_reduce(sm[:, t % 2, :], score[t % 2][:, 0:NK], mbias[:], DH ** -0.5, BIG,
                                         ALU.add, ALU.min, nmx[:, j % 2, t:t + 1]).then_inc(scores_masked, 1)

            def reciprocals(g, j, half):
                dve.wait_ge(exp_done, g * GB * NT + j * NT + 2 * half + 2)
                s = slice(2 * half, 2 * half + 2)
                dve.reciprocal(rsum[:, j % 2, s], ssum[:, j % 2, s]).then_inc(recip_done, 1)

            def prob_copy(g, j, half):
                dve.wait_ge(probT_full, 2 * (g * GB + j) + half + 1)
                if half == 0:
                    after(dve, ac_done, g * GB + j)
                dve.tensor_copy(prT[:, :, half * 256:(half + 1) * 256], probT[:].rearrange("p (m c) -> p m c", m=2)).then_inc(probT_copied, 1)

            def weighed(g, j):
                dve.wait_ge(ac_done, g * GB + j + 1)
                dve.tensor_copy(act_[:, :, j * NQ:(j + 1) * NQ],
                                ac_tail[:, 0:TOK].rearrange("p (n q) -> p n q", q=NQ)).then_inc(act_copied, 1)

            def aux_job(name, g):
                if name == "LT":
                    dve.wait_ge(aux_full, nth(AUX, name, g))
                    for r in range(4):
                        own = aux[0:NQ, r * NQ:(r + 1) * NQ].unsqueeze(1).broadcast_to([NQ, GB, NQ])
                        last = dve.tensor_tensor(spread[r * NQ:(r + 1) * NQ], own,
                                                 seqm[:].unsqueeze(2).broadcast_to([NQ, GB, NQ]), ALU.mult)
                    last.then_inc(aux_free, 1)

            def post_job(name, g):
                bank = post_bank(name, g) if name in POST else None
                if name[:2] == "OT" and name in ON_DVE:
                    n = int(name[2])
                    dve.wait_ge(post_full, nth(POST, name, g))
                    dve.tensor_copy(qT[:, 2 * n:2 * n + 2, :].rearrange("p n t -> p (n t)"), bank[:]).then_inc(post_copied["VectorE"], 1)
                elif name in ("WO0", "WO1"):
                    a = int(name[2])
                    dve.wait_ge(post_full, nth(POST, name, g))
                    dve.wait_ge(xb_ready, g + 1)
                    after(dve, y_ready, g)
                    dve.tensor_tensor(x1[:, a, :], bank[:, 0:DM], xb[:, a, :], ALU.add).then_inc(post_copied["VectorE"], 1)
                elif name[0] == "B":
                    if name == "B0":
                        dve.wait_ge(*copied("WO1", g))
                    layer_norm(1, int(name[1]), g, x1, hn, 1.0 + EPS, EPS * EPS)
                elif name[:2] == "KM":
                    a, c = divmod(int(name[2]), 2)
                    if name == "KM0":
                        dve.wait_ge(*copied("KT", g))
                    if name == "KM2":
                        dve.wait_ge(post_full, nth(POST, "SC0", g))
                    dve.tensor_tensor(kM[:, c], kT2[:, c, a * P:(a + 1) * P].unsqueeze(1).broadcast_to([P, 8, P]),
                                      headm[:].unsqueeze(2).broadcast_to([P, 8, P]), ALU.mult).then_inc(kM_ready, 1)
                elif name[:2] == "SC":
                    a = int(name[2])
                    dve.wait_ge(post_full, nth(POST, name, g))
                    rows = bank[:].rearrange("p (h k) -> p h k", k=NQ)
                    dve.tensor_reduce(smx[:, a, :], rows, AX.X, ALU.max).then_inc(smx_ready, 1)
                    dve.wait_ge(smx_ready, 2 * g + a + 1)
                    dve.tensor_tensor(sc[:, a], rows, smx[:, a, :].unsqueeze(2).broadcast_to([P, SH, NQ]),
                                      ALU.subtract).then_inc(post_copied["VectorE"], 1)
                elif name[:2] == "SM":
                    a = int(name[2])
                    dve.wait_ge(sexp_done, 2 * g + a + 1)
                    dve.tensor_reduce(ssm[:, a, :], sc[:, a], AX.X, ALU.add).then_inc(ssum_done, 1)
                    dve.wait_ge(ssum_done, 4 * g + 2 * a + 1)
                    dve.tensor_scalar(ssm[:, a, :], ssm[:, a, :], 1e-12, None, ALU.max).then_inc(ssum_done, 1)
                    dve.wait_ge(ssum_done, 4 * g + 2 * a + 2)
                    dve.reciprocal(rs2[:, a, :], ssm[:, a, :]).then_inc(srecip_done, 1)
                elif name == "VR":
                    dve.wait_ge(post_full, nth(POST, name, g))
                    for r in range(4):
                        rows = slice(r * NQ, (r + 1) * NQ)
                        last = dve.tensor_copy(vb[rows, :, :, r, :],
                                               bank[rows].rearrange("p (b c d) -> p b c d", b=GB, c=4))
                    last.then_inc(post_copied["VectorE"], 1)
                elif name == "PJ":
                    dve.wait_ge(post_full, nth(POST, name, g))
                    dve.wait_ge(x1b_ready, g + 1)
                    dve.tensor_tensor(x2[:].rearrange("p a c -> p (a c)"), bank[:], xb[:].rearrange("p a c -> p (a c)"),
                                      ALU.add).then_inc(post_copied["VectorE"], 1)
                elif name[0] == "C":
                    if name == "C0":
                        dve.wait_ge(*copied("PJ", g))
                    layer_norm(2, int(name[1]), g, x2, hn, 1.0, EPS)
                elif name == "M1":
                    for n, mu in enumerate((MUR, MUK)):
                        dve.wait_ge(half_mixed, 2 * g + n + 1)
                        for k in range(2):
                            last = dve.scalar_tensor_tensor(out=mix[:, 2 * n + k, :].rearrange("p (b q) -> p b q", q=NQ),
                                                            in0=x3T[:, k, :, 1:NQ + 1], scalar=cols[:, mu, k:k + 1],
                                                            in1=mixt[:, 2 * n + k, :].rearrange("p (b q) -> p b q", q=NQ),
                                                            op0=ALU.mult, op1=ALU.add)
                        last.then_inc(mixed, 1)
                elif name == "FR":
                    dve.wait_ge(post_full, nth(POST, name, g))
                    after(dve, y_ready, g)
                    dve.tensor_scalar(er.rearrange("p a c -> p (a c)"), bank[:], EXP_MAX, None, ALU.max).then_inc(post_copied["VectorE"], 1)
                elif name == "SG":
                    dve.wait_ge(er_exp, g + 1)
                    dve.tensor_scalar(er, er, 1.0, None, ALU.add).then_inc(er_one, 1)
                    dve.wait_ge(er_one, g + 1)
                    dve.reciprocal(er, er).then_inc(r_ready, 1)
                elif name == "FV":
                    dve.wait_ge(post_full, nth(POST, name, g))
                    dve.wait_ge(r_ready, g + 1)
                    dve.tensor_tensor(er.rearrange("p a c -> p (a c)"), bank[:], er.rearrange("p a c -> p (a c)"),
                                      ALU.mult).then_inc(post_copied["VectorE"], 1)

            def group(g, has_pre, has_post):
                for j, name, own in group_jobs(g, has_pre, has_post):
                    if name == "CT":
                        ctx_lower(next_sequence(g, j), *next_context(g, j))
                    elif name in ("S0", "S1", "S2", "S3"):
                        mask_scores(g, j, int(name[1]))
                    elif name in ("R0", "R1"):
                        half = int(name[1])
                        reciprocals(g, j - half, half)
                    elif name in ("CL", "L0", "L1"):
                        lower_parts(dve, name, g, j, name in LOWER_ON_DVE)
                    elif name in ("P0", "P1"):
                        if name in ON_DVE:
                            prob_copy(g, j - 1, int(name[1]))
                    elif name == "AC":
                        weighed(g, j - 1)
                    elif name == "LT":
                        aux_job(name, g)
                    elif name in FOR_PRE:
                        if name[0] == "A":
                            norm_input(int(name[1]), own)
                        elif name[0] == "K":
                            qk_lower(int(name[1:]), own)
                    elif name not in CORE:
                        post_job(name, own)

            for stage in range(5):
                norm_input(stage, 0)
            dve.wait_ge(left_upper, 1)
            dve.tensor_tensor(left_l[:].rearrange("p k b -> p (k b)"), wk_bank[0][:, 2 * DC:2 * DC + 2 * NB],
                              left_h[:].rearrange("p k b -> p (k b)"), ALU.subtract).then_inc(setup_copied, 1)
            dve.wait_ge(zeroed, 1)
            for n in range(4):
                dve.wait_ge(setup_full, SETUP_TRANSPOSES.index(f"WK{n}") + 1)
                src = wk_bank[n][:, 0:2 * DC].rearrange("p (i c) -> p i c", i=2)
                for r in range(2):
                    half = slice(r * 64, r * 64 + 64)
                    dst = nwk[half].rearrange("p (n r) c -> p n r c", r=2)[:, 2 * n:2 * n + 2, r, :]
                    dve.tensor_scalar(dst, src[half, :, 0:P], -1.0, None, ALU.mult)
                    last = dve.tensor_scalar(nwkt[half, 2 * n:2 * n + 2, r * 64:r * 64 + 64], src[half, :, P:DC], -1.0, None, ALU.mult)
                last.then_inc(setup_copied, 1)
            dve.wait_ge(ident_made, 2)
            dve.tensor_reduce(headm[:], ident[:].rearrange("p (h d) -> p h d", d=16), AX.X, ALU.add).then_inc(consts_made, 1)
            dve.tensor_reduce(seqm[:], ident[0:NQ, 0:NQ].rearrange("p (t b) -> p b t", b=GB), AX.X, ALU.add).then_inc(consts_made, 1)
            dve.tensor_reduce(leftm[:], ident[:].rearrange("p (r t b) -> p t r b", r=4, b=GB), AX.X, ALU.add).then_inc(consts_made, 1)
            dve.wait_ge(mask_in, 64)
            dve.tensor_reduce(poison[:, 1:2], mraw[:], AX.X, ALU.max).then_inc(consts_made, 1)
            dve.tensor_scalar(mbias[:], mraw[:], -MASKED, MASKED, ALU.mult, ALU.add).then_inc(consts_made, 1)
            dve.wait_ge(consts_made, 5)
            dve.reciprocal(poison[:, 0:1], poison[:, 1:2]).then_inc(consts_made, 1)
            dve.wait_ge(consts_made, 6)
            dve.tensor_tensor(poison[:, 0:1], poison[:, 0:1], poison[:, 1:2], ALU.mult).then_inc(consts_made, 1)
            dve.wait_ge(small_in, 16 * N_SMALL)
            dve.tensor_scalar(cols[:, MUR1:MUK1 + 1, :], cols[:, MUR:MUK + 1, :], -1.0, 1.0, ALU.mult, ALU.add).then_inc(consts_made, 1)
            dve.wait_ge(consts_made, 8)
            for n in range(len(QK)):
                if n == 9:
                    ctx_lower(0, "CT0", 0)
                qk_lower(n, 0)
            groups(dve, group)
            for name in CLOSING:
                post_job(name, NG - 1)


_INS = ["x", "ctx_768", "mask_1x1xSxS2_bk0", "L0_xattn_ln_gamma", "L0_xattn_ln_beta", "L0_xattn_Wq", "L0_xattn_Wkv",
        "L0_xattn_Wo", "L0_xattn_bo", "L0_attn_ln_gamma", "L0_attn_ln_beta", "L0_attn_W_qkv", "L0_attn_b_qkv",
        "L0_attn_W_proj", "L0_attn_b_proj", "L0_ffn_W_r", "L0_ffn_W_k", "L0_ffn_W_v", "L0_ffn_mu_r", "L0_ffn_mu_k"]
_OUTS = [((NB, NQ, DM), "float32")]


def kernel(**inputs):
    import numpy as _np
    import concourse.bacc as _bacc
    from concourse import mybir as _mybir
    from concourse.bass_utils import run_bass_kernel_spmd as _run

    nc = _bacc.Bacc("TRN2", target_bir_lowering=False, num_devices=1, dynamic_dma_scratch_size=256)
    arrays, args = {}, []
    for name in _INS:
        a = _np.ascontiguousarray(inputs[name])
        arrays[f"in_{name}_dram"] = a
        args.append(nc.dram_tensor(f"in_{name}_dram", a.shape, _mybir.dt.from_np(a.dtype), kind="ExternalInput").ap())
    for i, (shape, dtype) in enumerate(_OUTS):
        dt = _mybir.dt.from_np(_np.dtype(dtype))
        args.append(nc.dram_tensor(f"out_{i}_dram", shape, dt, kind="ExternalOutput").ap())
    perceiver_layer(nc, *args)
    r = _run(nc, [arrays], core_ids=[0])
    return r.results[0]["out_0_dram"]
```
